# Optimizing a Trainium2 kernel written in Bass

```python
import numpy as np
import jax
import jax.numpy as jnp

def _softmax(x, axis=-1):
    return jax.nn.softmax(x, axis=axis)

def _gelu(x):
    return jax.nn.gelu(x, approximate=True)

def _silu(x):
    return jax.nn.silu(x)

def _sigmoid(x):
    return jax.nn.sigmoid(x)

def _layernorm(x, axis=-1, eps=1e-05):
    m = jnp.mean(x, axis=axis, keepdims=True)
    v = jnp.var(x, axis=axis, keepdims=True)
    return (x - m) / jnp.sqrt(v + eps)

def _scatter_add(tgt, idx, src, axis=0):
    return tgt.at[idx].add(src)

def _segment_sum(src, seg, n):
    return jax.ops.segment_sum(src, seg, n)
kernel_name = 'mk_prb_d2_jaxref_r8_4bf721'

def setup_inputs(seed: int=0):
    np.random.seed(seed)
    _w = jnp.asarray

    def _L0_attn_setup():
        import jax, jax.numpy as jnp
        import numpy as np
        H = 512
        D = H // 4
        key = jax.random.key(seed)
        k1, k2, k3, k4, k5 = jax.random.split(key, 5)
        x = jax.random.normal(k1, (4, 512, H), dtype=jnp.float32)
        s_in = 1.0 / np.sqrt(H)
        Wqkv = jax.random.normal(k2, (H, 3 * D), dtype=jnp.float32) * s_in
        bqkv = jax.random.normal(k3, (3 * D,), dtype=jnp.float32) * 0.01
        Wo = jax.random.normal(k4, (D, H), dtype=jnp.float32) * (1.0 / np.sqrt(D))
        bo = jax.random.normal(k5, (H,), dtype=jnp.float32) * 0.01
        return {'x': x, 'Wqkv': Wqkv, 'bqkv': bqkv, 'Wo': Wo, 'bo': bo}
    _L0_attn_in = _L0_attn_setup()

    def _L0_ffn_setup():
        import jax, jax.numpy as jnp
        import numpy as np
        N_STREAMS = 4
        DIM = 128
        SINKHORN_ITERS = 50
        SINKHORN_TAU = 0.1
        RMS_EPS = 1.1920929e-07

        def sinkhorn_log(logits, num_iters=SINKHORN_ITERS, tau=SINKHORN_TAU):
            Z = logits / tau
            u0 = jnp.zeros(Z.shape[:-1], Z.dtype)
            v0 = jnp.zeros_like(u0)

            def step(carry, _):
                u, v = carry
                u = -jax.nn.logsumexp(Z + v[..., None, :], axis=-1)
                v = -jax.nn.logsumexp(Z + u[..., :, None], axis=-2)
                return ((u, v), None)
            (u, v), _ = jax.lax.scan(step, (u0, v0), None, length=num_iters)
            return jnp.exp(Z + u[..., :, None] + v[..., None, :])
        key = jax.random.key(seed)
        ks = jax.random.split(key, 6)
        B, T = (4, 256)
        n, C = (N_STREAMS, DIM)
        wd = n * C
        x = jax.random.normal(ks[0], (B, T, wd), dtype=jnp.float32)
        W_res = 0.01 * jax.random.normal(ks[1], (n * n, wd), dtype=jnp.float32)
        W_pre = 0.01 * jax.random.normal(ks[2], (n, wd), dtype=jnp.float32)
        W_post = 0.01 * jax.random.normal(ks[3], (n, wd), dtype=jnp.float32)
        H_res_base = jnp.full((n, n), -0.5, dtype=jnp.float32)
        H_res_base = H_res_base.at[jnp.arange(n), jnp.arange(n)].set(0.0)
        H_pre_base = jnp.zeros((n,), dtype=jnp.float32).at[0].set(1.0)
        H_post_base = jnp.zeros((n,), dtype=jnp.float32)
        gate = jnp.array([5.0], dtype=jnp.float32)
        W_branch = 1.0 / np.sqrt(C) * jax.random.normal(ks[4], (C, C), dtype=jnp.float32)
        return {'x': x, 'W_res': W_res, 'W_pre': W_pre, 'W_post': W_post, 'H_res_base': H_res_base, 'H_pre_base': H_pre_base, 'H_post_base': H_post_base, 'gate': gate, 'W_branch': W_branch}
    _L0_ffn_in = _L0_ffn_setup()

    def _L1_attn_setup():
        import jax, jax.numpy as jnp
        import numpy as np
        B, S, HID = (1, 256, 512)
        H, HK, D = (32, 8, 128)
        L = D // 4
        key = jax.random.key(seed)
        ks = jax.random.split(key, 7)
        s = 0.02
        return {'hidden_states': jax.random.normal(ks[0], (B, S, HID), jnp.float32), 'Wq': jax.random.normal(ks[1], (H * D, HID), jnp.float32) * s, 'Wk_down': jax.random.normal(ks[2], (HK * L, HID), jnp.float32) * s, 'Wv_down': jax.random.normal(ks[3], (HK * L, HID), jnp.float32) * s, 'Wk_up': jax.random.normal(ks[4], (HK * D, HK * L), jnp.float32) * s, 'Wv_up': jax.random.normal(ks[5], (HK * D, HK * L), jnp.float32) * s, 'Wo': jax.random.normal(ks[6], (HID, H * D), jnp.float32) * s}
    _L1_attn_in = _L1_attn_setup()

    def _L1_ffn_setup():
        import jax, jax.numpy as jnp
        import numpy as np
        B, S, IN, OUT = (4, 256, 512, 512)
        E, K, R = (8, 2, 16)
        CAP_FACTOR = 3.0
        ALPHA = 1.0 / R
        LN_EPS = 1e-05
        key = jax.random.key(seed)
        ks = jax.random.split(key, 6)
        return {'x': jax.random.normal(ks[0], (B, S, IN), dtype=jnp.float32), 'weight': jax.random.normal(ks[1], (OUT, IN), dtype=jnp.float32) * 0.02, 'lora_A': jax.random.normal(ks[2], (E, IN, R), dtype=jnp.float32) / np.sqrt(R), 'lora_B': jax.random.normal(ks[3], (E, R, OUT), dtype=jnp.float32) * 0.02, 'gw1': jax.random.normal(ks[4], (4 * E, IN), dtype=jnp.float32) * 0.02, 'gb1': jnp.zeros((4 * E,), dtype=jnp.float32), 'ln_gamma': jnp.ones((4 * E,), dtype=jnp.float32), 'ln_beta': jnp.zeros((4 * E,), dtype=jnp.float32), 'gw2': jax.random.normal(ks[5], (E, 4 * E), dtype=jnp.float32) * 0.02, 'gb2': jnp.zeros((E,), dtype=jnp.float32)}
    _L1_ffn_in = _L1_ffn_setup()
    _d = {'L0_attn_x': _L0_attn_in['x'], 'L0_attn_Wqkv': _L0_attn_in['Wqkv'], 'L0_attn_bqkv': _L0_attn_in['bqkv'], 'L0_attn_Wo': _L0_attn_in['Wo'], 'L0_attn_bo': _L0_attn_in['bo'], 'L0_ffn_W_res': _L0_ffn_in['W_res'], 'L0_ffn_W_pre': _L0_ffn_in['W_pre'], 'L0_ffn_W_post': _L0_ffn_in['W_post'], 'L0_ffn_H_res_base': _L0_ffn_in['H_res_base'], 'L0_ffn_H_pre_base': _L0_ffn_in['H_pre_base'], 'L0_ffn_H_post_base': _L0_ffn_in['H_post_base'], 'L0_ffn_gate': _L0_ffn_in['gate'], 'L0_ffn_W_branch': _L0_ffn_in['W_branch'], 'L1_attn_Wq': _L1_attn_in['Wq'], 'L1_attn_Wk_down': _L1_attn_in['Wk_down'], 'L1_attn_Wv_down': _L1_attn_in['Wv_down'], 'L1_attn_Wk_up': _L1_attn_in['Wk_up'], 'L1_attn_Wv_up': _L1_attn_in['Wv_up'], 'L1_attn_Wo': _L1_attn_in['Wo'], 'L1_ffn_weight': _L1_ffn_in['weight'], 'L1_ffn_lora_A': _L1_ffn_in['lora_A'], 'L1_ffn_lora_B': _L1_ffn_in['lora_B'], 'L1_ffn_gw1': _L1_ffn_in['gw1'], 'L1_ffn_gb1': _L1_ffn_in['gb1'], 'L1_ffn_ln_gamma': _L1_ffn_in['ln_gamma'], 'L1_ffn_ln_beta': _L1_ffn_in['ln_beta'], 'L1_ffn_gw2': _L1_ffn_in['gw2'], 'L1_ffn_gb2': _L1_ffn_in['gb2']}
    _x0 = _d['L0_attn_x']
    _d['L0_attn_x'] = jax.random.normal(jax.random.fold_in(jax.random.key(seed), 1), (2, 1024, 512), dtype=_x0.dtype)
    del _x0
    return _d

def reference(L0_attn_x, L0_attn_Wqkv, L0_attn_bqkv, L0_attn_Wo, L0_attn_bo, L0_ffn_W_res, L0_ffn_W_pre, L0_ffn_W_post, L0_ffn_H_res_base, L0_ffn_H_pre_base, L0_ffn_H_post_base, L0_ffn_gate, L0_ffn_W_branch, L1_attn_Wq, L1_attn_Wk_down, L1_attn_Wv_down, L1_attn_Wk_up, L1_attn_Wv_up, L1_attn_Wo, L1_ffn_weight, L1_ffn_lora_A, L1_ffn_lora_B, L1_ffn_gw1, L1_ffn_gb1, L1_ffn_ln_gamma, L1_ffn_ln_beta, L1_ffn_gw2, L1_ffn_gb2):

    def _L0_attn_ref(x, Wqkv, bqkv, Wo, bo):
        import jax, jax.numpy as jnp
        import numpy as np
        H = 512
        D = H // 4
        B, S, C = x.shape
        d = C // 4
        qkv = jnp.einsum('bsc,cf->bsf', x, Wqkv) + bqkv
        qkv = qkv.reshape(B, S, 3, d)
        q, k, v = (qkv[:, :, 0], qkv[:, :, 1], qkv[:, :, 2])
        scale = 1.0 / jnp.sqrt(jnp.float32(d)).astype(x.dtype)
        attn = jnp.einsum('bqd,bkd->bqk', q, k) * scale
        attn = jax.nn.softmax(attn, axis=-1)
        out = jnp.einsum('bqk,bkd->bqd', attn, v)
        return jnp.einsum('bqd,dc->bqc', out, Wo) + bo

    def _L0_ffn_ref(x, W_res, W_pre, W_post, H_res_base, H_pre_base, H_post_base, gate, W_branch):
        import jax, jax.numpy as jnp
        import numpy as np
        N_STREAMS = 4
        DIM = 128
        SINKHORN_ITERS = 50
        SINKHORN_TAU = 0.1
        RMS_EPS = 1.1920929e-07

        def sinkhorn_log(logits, num_iters=SINKHORN_ITERS, tau=SINKHORN_TAU):
            Z = logits / tau
            u0 = jnp.zeros(Z.shape[:-1], Z.dtype)
            v0 = jnp.zeros_like(u0)

            def step(carry, _):
                u, v = carry
                u = -jax.nn.logsumexp(Z + v[..., None, :], axis=-1)
                v = -jax.nn.logsumexp(Z + u[..., :, None], axis=-2)
                return ((u, v), None)
            (u, v), _ = jax.lax.scan(step, (u0, v0), None, length=num_iters)
            return jnp.exp(Z + u[..., :, None] + v[..., None, :])
        B, T, nC = x.shape
        n = N_STREAMS
        C = nC // n
        x_norm = x * jax.lax.rsqrt(jnp.mean(x * x, axis=-1, keepdims=True) + RMS_EPS)
        H_res_logits = (x_norm @ W_res.T).reshape(B, T, n, n) + H_res_base
        H_pre_logits = x_norm @ W_pre.T + H_pre_base
        H_post_logits = x_norm @ W_post.T + H_post_base
        H_res = sinkhorn_log(H_res_logits)
        H_pre = jax.nn.softmax(H_pre_logits, axis=-1)
        H_post = jax.nn.softmax(H_post_logits, axis=-1)
        g = jax.nn.sigmoid(gate)[0]
        I = jnp.eye(n, dtype=H_res.dtype)
        H_res = (1.0 - g) * I + g * H_res
        x_streams = x.reshape(B, T, n, C)
        x_pre = jnp.einsum('btnc,btn->btc', x_streams, H_pre)
        y = x_pre @ W_branch
        x_mixed = jnp.einsum('btij,btjc->btic', H_res, x_streams)
        y_distributed = jnp.einsum('btc,btn->btnc', y, H_post)
        return (x_mixed + y_distributed).reshape(B, T, nC)

    def _L1_attn_ref(hidden_states, Wq, Wk_down, Wv_down, Wk_up, Wv_up, Wo):
        import jax, jax.numpy as jnp
        import numpy as np
        B, S, HID = (1, 256, 512)
        H, HK, D = (32, 8, 128)
        L = D // 4
        b, s, _ = hidden_states.shape
        q = (hidden_states @ Wq.T).reshape(b, s, H, D).transpose(0, 2, 1, 3)
        kc = (hidden_states @ Wk_down.T).reshape(b, s, HK, L).transpose(0, 2, 1, 3)
        vc = (hidden_states @ Wv_down.T).reshape(b, s, HK, L).transpose(0, 2, 1, 3)
        lat = jnp.concatenate([kc, vc], axis=-1).reshape(b, s, HK * 2 * L)
        k_cmp, v_cmp = jnp.split(lat, 2, axis=-1)
        k = (k_cmp @ Wk_up.T).reshape(b, s, HK, D).transpose(0, 2, 1, 3)
        v = (v_cmp @ Wv_up.T).reshape(b, s, HK, D).transpose(0, 2, 1, 3)
        n_rep = H // HK
        k = jnp.repeat(k, n_rep, axis=1)
        v = jnp.repeat(v, n_rep, axis=1)
        scale = 1.0 / jnp.sqrt(jnp.asarray(D, hidden_states.dtype))
        scores = jnp.einsum('bhqd,bhkd->bhqk', q, k) * scale
        causal = jnp.tril(jnp.ones((s, s), dtype=bool))
        scores = jnp.where(causal, scores, jnp.asarray(-1000000000.0, scores.dtype))
        attn = jax.nn.softmax(scores, axis=-1)
        out = jnp.einsum('bhqk,bhkd->bhqd', attn, v)
        out = out.transpose(0, 2, 1, 3).reshape(b, s, H * D)
        return out @ Wo.T

    def _L1_ffn_ref(x, weight, lora_A, lora_B, gw1, gb1, ln_gamma, ln_beta, gw2, gb2):
        import jax, jax.numpy as jnp
        import numpy as np
        B, S, IN, OUT = (4, 256, 512, 512)
        E, K, R = (8, 2, 16)
        CAP_FACTOR = 3.0
        ALPHA = 1.0 / R
        LN_EPS = 1e-05
        orig_shape = x.shape
        xf = x.reshape(-1, orig_shape[-1])
        N = xf.shape[0]
        capacity = int(CAP_FACTOR * N / E)
        h = xf @ gw1.T + gb1
        mu = jnp.mean(h, axis=-1, keepdims=True)
        var = jnp.mean((h - mu) ** 2, axis=-1, keepdims=True)
        h = (h - mu) * jax.lax.rsqrt(var + LN_EPS) * ln_gamma + ln_beta
        h = jax.nn.relu(h)
        gates = h @ gw2.T + gb2
        top_v, top_i = jax.lax.top_k(gates, K)
        top_g = jax.nn.softmax(top_v, axis=-1)
        onehot = (top_i[..., None] == jnp.arange(E)).astype(xf.dtype)
        counts = onehot.sum(axis=0)
        allowed = (counts <= capacity).astype(xf.dtype)
        w = jnp.einsum('nke,nk,ke->ne', onehot, top_g, allowed)
        main = xf @ weight.T
        tmp = jnp.einsum('ni,eir->enr', xf, lora_A)
        tmp = tmp * w.T[:, :, None]
        lora = jnp.einsum('enr,ero->no', tmp, lora_B) * ALPHA
        out = main + lora
        return out.reshape(*orig_shape[:-1], weight.shape[0])
    x = L0_attn_x
    xn = _layernorm(x, axis=-1)
    x = x + _L0_attn_ref(xn, L0_attn_Wqkv, L0_attn_bqkv, L0_attn_Wo, L0_attn_bo) + _L0_ffn_ref(xn, L0_ffn_W_res, L0_ffn_W_pre, L0_ffn_W_post, L0_ffn_H_res_base, L0_ffn_H_pre_base, L0_ffn_H_post_base, L0_ffn_gate, L0_ffn_W_branch)
    xn = _layernorm(x, axis=-1)
    x = x + _L1_attn_ref(xn, L1_attn_Wq, L1_attn_Wk_down, L1_attn_Wv_down, L1_attn_Wk_up, L1_attn_Wv_up, L1_attn_Wo) + _L1_ffn_ref(xn, L1_ffn_weight, L1_ffn_lora_A, L1_ffn_lora_B, L1_ffn_gw1, L1_ffn_gb1, L1_ffn_ln_gamma, L1_ffn_ln_beta, L1_ffn_gw2, L1_ffn_gb2)
    return x

_drawn_inputs = setup_inputs


def setup_inputs(seed=0):
    import zlib

    import numpy as np

    out = dict(_drawn_inputs(seed))
    spreads = {'L0_ffn_H_post_base': (0.0, 0.8),
     'L1_ffn_gb1': (0.0, 2.0),
     'L1_ffn_ln_gamma': (1.0, 0.6),
     'L1_ffn_ln_beta': (0.0, 2.0),
     'L1_ffn_gb2': (0.0, 2.0)}
    factors = {'L0_attn_bqkv': 8.0,
     'L0_attn_bo': 8.0,
     'L0_ffn_W_pre': 4.344,
     'L0_ffn_W_post': 4.055,
     'L1_attn_Wq': 8.0,
     'L1_attn_Wk_down': 8.0,
     'L1_attn_Wv_down': 8.0,
     'L1_attn_Wk_up': 8.0,
     'L1_attn_Wv_up': 6.786,
     'L1_attn_Wo': 6.885,
     'L1_ffn_lora_A': 42.73,
     'L1_ffn_lora_B': 43.162,
     'L1_ffn_gw1': 57.729,
     'L1_ffn_gw2': 50.81,
     'L1_ffn_weight': 7.821}
    for name, (base, spread) in spreads.items():
        noise = np.random.default_rng([zlib.crc32(name.encode()), seed]).standard_normal(out[name].shape)
        drawn = base * np.exp(spread * noise) if base else spread * noise
        out[name] = jnp.asarray(drawn.astype(out[name].dtype))
    for name, factor in factors.items():
        out[name] = (out[name] * factor).astype(out[name].dtype)
    return out
```

```python
from contextlib import ExitStack

import concourse.bass as bass
from concourse import mybir

F32 = mybir.dt.float32
F32R = mybir.dt.float32r
BF16 = mybir.dt.bfloat16
ALU = mybir.AluOpType
ACT = mybir.ActivationFunctionType
AX = mybir.AxisListType

P = 128
B, S, HID = 2, 1024, 512
N = B * S
NT = N // P
TB = S // P
CH = HID // P
D = 128
LN_EPS = 1e-5
RMS_EPS = 1.1920929e-07
NS = 4
NZ = NS * NS
NLOG = NZ + 2 * NS
TAU = 0.1
SINKHORN_ITERS = 50
SINKHORN_CHUNK = 25
HEADS, KV_HEADS = 32, 8
REP = HEADS // KV_HEADS
LAT = D // 4
ATT = HEADS * D
LATW = KV_HEADS * LAT
LC = LATW // P
KVW = KV_HEADS * D
EXP, TOPK, RANK = 8, 2, 16
GH = 4 * EXP
ALPHA = 1.0 / RANK
CAPACITY = int(3.0 * N / EXP)
SCALE = float(D) ** -0.5
MASKED = -1e30


class Shared:
    pass


def mm3(pe, out, terms, start=True, stop=True):
    n = len(terms)
    for i, (wh, wl, xh, xl) in enumerate(terms):
        pe.matmul(out, wh, xh, start=start and i == 0, stop=False)
        pe.matmul(out, wh, xl, start=False, stop=False)
        last = pe.matmul(out, wl, xh, start=False, stop=stop and i == n - 1)
    return last


def f32(ap):
    return ap.bitcast(F32)


def layer0_project(nc, a, m, bank):
    with ExitStack() as ctx:
        def sb(name, shape, dt=F32):
            return ctx.enter_context(nc.sbuf_tensor(name, shape, dt))

        def pair(name, shape):
            return sb(name + "_h", shape, F32R), sb(name + "_l", shape, F32R)

        def sem(name):
            return ctx.enter_context(nc.semaphore(name))

        xT0_h, xT0_l = pair("xT0", [P, CH, N])
        wqkv = m.xn0[:, NT - 3:NT, :].rearrange("p t c -> p (t c)").rearrange("p (c f) -> p c f", c=CH)
        wqkv2_h, wqkv2_l = pair("wqkv2", [P, CH, 3 * D])
        wlog = sb("wlog", [NLOG, HID])
        wlogT_h, wlogT_l = pair("wlogT", [P, CH, P])
        bqkv = sb("bqkv", [P, 3])
        bo = sb("bo", [P, HID])
        zbase = sb("zbase", [P, NLOG])
        st = sb("st0", [P, NT, 6])
        mv = sb("mv0", [P, NT, 2])
        rstd = sb("rstd0", [P, NT])
        ssq = sb("ssq0", [P, NT])
        rms = sb("rms0", [P, NT])
        tmpv = sb("tmpv0", [P, 2, NT])
        mhalf = sb("mhalf0", [P, NT])
        junk = sb("junk0", [P, HID], BF16)
        vT = sb("vT0", [P, 512])
        lgT = sb("lgT0", [NLOG, 512])
        xn, x1 = m.xn0, m.acc

        x_in = [sem(f"a_x_in{n}") for n in range(4)]
        w_in, const = sem("a_w_in"), sem("a_const")
        st_done, mv_done, var_eps, rstd_ok, xn_ok = sem("a_st"), sem("a_mv"), sem("a_var"), sem("a_rstd"), sem("a_xn")
        ssq_ok, rms_in, rms_ok, xbo = sem("a_ssq"), sem("a_rmsin"), sem("a_rms"), sem("a_xbo")
        wl_mm, wl_hi, wl_lo, wq_hi, wq_lo = sem("a_wlmm"), sem("a_wlhi"), sem("a_wllo"), sem("a_wqhi"), sem("a_wqlo")
        xT_mm, xT_hi, xT_lo = sem("a_xTmm"), sem("a_xThi"), sem("a_xTlo")
        job_mm, qk_hi, qk_lo = sem("a_jobmm"), sem("a_qkhi"), sem("a_qklo")
        vT_ok, lgT_ok = sem("a_vT"), sem("a_lgT")
        v_mm, v_hi, v_lo, lg_mm, lg_ok = sem("a_vmm"), sem("a_vhi"), sem("a_vlo"), sem("a_lgmm"), sem("a_lg")
        TQ = 4
        W_LOADS = 11

        block = ctx.enter_context(nc.Block())

        @block.sync
        def _(sp):
            for n in range(4):
                sp.dma_start(x1[:, TQ * n:TQ * n + TQ, :],
                             a["L0_attn_x"].rearrange("b s c -> (b s) c")[512 * n:512 * n + 512, :]
                             .rearrange("(t p) c -> p t c", p=P)).then_inc(x_in[n], 16)

        @block.gpsimd
        def _(pool):
            pool.memset(m.ident[:], 0.0).then_inc(const, 1)
            pool.memset(m.maskb[:], 0.0).then_inc(const, 1)
            pool.memset(m.ones[:], 1.0).then_inc(const, 1)
            pool.memset(mhalf[:], -0.5).then_inc(const, 1)
            pool.memset(f32(wlogT_h[:]), 0.0).then_inc(const, 1)
            pool.memset(f32(wlogT_l[:]), 0.0).then_inc(const, 1)
            pool.wait_ge(const, 6)
            pool.affine_select(out=m.ident[:], in_=m.ident[:], compare_op=ALU.not_equal, fill=1.0,
                               base=0, pattern=[[-1, P]], channel_multiplier=1).then_inc(const, 1)
            pool.affine_select(out=m.maskb[:], in_=m.maskb[:], compare_op=ALU.is_ge, fill=MASKED,
                               base=0, pattern=[[-1, P]], channel_multiplier=1).then_inc(const, 1)
            pool.wait_ge(const, 8)
            pool.tensor_copy(m.identb[:], m.ident[:]).then_inc(const, 1)
            pool.wait_ge(wq_hi, 1)
            pool.tensor_tensor(wqkv2_l[:], wqkv, f32(wqkv2_h[:]), ALU.subtract).then_inc(wq_lo, 1)

            def rms_of(n):
                cols = slice(TQ * n, TQ * n + TQ)
                pool.wait_ge(ssq_ok, TQ * (n + 1))
                pool.tensor_scalar(tmpv[:, 1, cols], ssq[:, cols], 1.0 / HID, RMS_EPS, ALU.mult,
                                   ALU.add).then_inc(rms_in, 1)
                pool.wait_ge(rms_in, n + 1)
                pool.tensor_tensor(rms[:, cols], tmpv[:, 1, cols], mhalf[:, cols], ALU.pow).then_inc(rms_ok, 1)

            for n in range(4):
                cols = slice(TQ * n, TQ * n + TQ)
                pool.wait_ge(mv_done, TQ * (n + 1))
                pool.tensor_scalar(tmpv[:, 0, cols], mv[:, cols, 1], 1.0, LN_EPS, ALU.mult,
                                   ALU.add).then_inc(var_eps, 1)
                pool.wait_ge(var_eps, n + 1)
                pool.tensor_tensor(rstd[:, cols], tmpv[:, 0, cols], mhalf[:, cols], ALU.pow).then_inc(rstd_ok, 1)
                if n:
                    rms_of(n - 1)
            rms_of(3)
            pool.wait_ge(w_in, 16 * W_LOADS)
            for t in range(NT):
                pool.wait_ge(xn_ok, t + 1)
                pool.tensor_tensor(x1[:, t, :], x1[:, t, :], bo[:], ALU.add).then_inc(xbo, 1)

        @block.vector
        def _(dve):
            def stats(n):
                dve.wait_ge(x_in[n], 16)
                for t in range(TQ * n, TQ * n + TQ):
                    dve.bn_stats(st[:, t, :], x1[:, t, :]).then_inc(st_done, 1)
                for t in range(TQ * n, TQ * n + TQ):
                    dve.wait_ge(st_done, t + 1)
                    dve.bn_aggr(mv[:, t, :], st[:, t, :]).then_inc(mv_done, 1)

            def norm(n):
                dve.wait_ge(rstd_ok, n + 1)
                if n == 3:
                    dve.wait_ge(wq_lo, 1)
                for t in range(TQ * n, TQ * n + TQ):
                    if t == TQ * n:
                        dve.wait_ge(mv_done, TQ * n + TQ)
                    dve.tensor_scalar(xn[:, t, :], x1[:, t, :], mv[:, t, 0:1], rstd[:, t:t + 1], ALU.subtract,
                                      ALU.mult).then_inc(xn_ok, 1)

            def low_xT(n):
                for t in range(TQ * n, TQ * n + TQ):
                    dve.wait_ge(xT_hi, t + 1)
                    cols = slice(t * P, t * P + P)
                    dve.tensor_tensor(xT0_l[:, :, cols], bank[t % 2][:].rearrange("p (c t) -> p c t", c=CH),
                                      f32(xT0_h[:, :, cols]), ALU.subtract).then_inc(xT_lo, 1)

            def low_qk(n):
                cols = slice(512 * n, 512 * n + 512)
                for k, (h, l) in enumerate(((m.q0_h, m.q0_l), (m.k0_h, m.k0_l))):
                    dve.wait_ge(qk_hi, 2 * n + k + 1)
                    dve.scalar_tensor_tensor(out=l[:, cols], in0=bank[2 + k][:], scalar=bqkv[:, k:k + 1],
                                             in1=f32(h[:, cols]), op0=ALU.add, op1=ALU.subtract).then_inc(qk_lo, 1)

            def post(n):
                dve.wait_ge(v_hi, n + 1)
                tiles = slice(TQ * n, TQ * n + TQ)
                dve.tensor_tensor(m.v0_l[:, tiles, :], bank[6][:].rearrange("p (t d) -> p t d", t=TQ),
                                  f32(m.v0_h[:, tiles, :]), ALU.subtract).then_inc(v_lo, 1)
                dve.wait_ge(rms_ok, n + 1)
                dve.wait_ge(lg_mm, n + 1)
                for k in range(TQ):
                    t = TQ * n + k
                    dve.scalar_tensor_tensor(out=m.logits[:, t, :], in0=bank[7][:, k * NLOG:(k + 1) * NLOG],
                                             scalar=rms[:, t:t + 1], in1=zbase[:], op0=ALU.mult,
                                             op1=ALU.add).then_inc(lg_ok, 1)

            stats(0)
            dve.wait_ge(w_in, 16 * W_LOADS)
            dve.wait_ge(wl_hi, 1)
            dve.tensor_tensor(wlogT_l[:, :, 0:NLOG], bank[7][:, 0:CH * NLOG].rearrange("p (c n) -> p c n", c=CH),
                              f32(wlogT_h[:, :, 0:NLOG]), ALU.subtract).then_inc(wl_lo, 1)
            for s in range(6):
                if s < 3:
                    stats(s + 1)
                if s < 4:
                    norm(s)
                    low_xT(s)
                if 1 <= s <= 4:
                    low_qk(s - 1)
                if s >= 2:
                    post(s - 2)

        @block.scalar
        def _(act):
            for dst, src in ((wqkv, a["L0_attn_Wqkv"].rearrange("(c p) f -> p c f", p=P)),
                             (wlog[0:NZ, :], a["L0_ffn_W_res"]), (wlog[NZ:NZ + NS, :], a["L0_ffn_W_pre"]),
                             (wlog[NZ + NS:NLOG, :], a["L0_ffn_W_post"]),
                             *((bqkv[:, k:k + 1], a["L0_attn_bqkv"][k * D:k * D + D].rearrange("(d o) -> d o", o=1))
                               for k in range(3)),
                             (bo[:], a["L0_attn_bo"].partition_broadcast(P)),
                             (zbase[:, 0:NZ], a["L0_ffn_H_res_base"].rearrange("i j -> (i j)").partition_broadcast(P)),
                             (zbase[:, NZ:NZ + NS], a["L0_ffn_H_pre_base"].partition_broadcast(P)),
                             (zbase[:, NZ + NS:NLOG], a["L0_ffn_H_post_base"].partition_broadcast(P))):
                act.dma_start(dst, src).then_inc(w_in, 16)
            act.wait_ge(w_in, 16 * W_LOADS)
            act.activation(wqkv2_h[:], wqkv, ACT.Copy).then_inc(wq_hi, 1)
            act.wait_ge(const, 6)
            act.wait_ge(wl_mm, 1)
            act.activation(wlogT_h[:, :, 0:NLOG], bank[7][:, 0:CH * NLOG].rearrange("p (c n) -> p c n", c=CH),
                           ACT.Copy).then_inc(wl_hi, 1)

            def high_xT(n):
                for t in range(TQ * n, TQ * n + TQ):
                    act.wait_ge(xT_mm, t + 1)
                    act.activation(xT0_h[:, :, t * P:t * P + P], bank[t % 2][:].rearrange("p (c t) -> p c t", c=CH),
                                   ACT.Copy).then_inc(xT_hi, 1)
                for t in range(TQ * n, TQ * n + TQ):
                    act.wait_ge(xn_ok, t + 1)
                    if t:
                        act.wait_ge(ssq_ok, t)
                    act.activation(junk[:], xn[:, t, :], ACT.Square, accum_out=ssq[:, t:t + 1]).then_inc(ssq_ok, 1)

            def jobs(n):
                cols = slice(512 * n, 512 * n + 512)
                for k, h in enumerate((m.q0_h, m.k0_h)):
                    act.wait_ge(job_mm, 4 * n + k + 1)
                    act.activation(h[:, cols], bank[2 + k][:], ACT.Identity, bias=bqkv[:, k:k + 1]).then_inc(qk_hi, 1)
                act.wait_ge(job_mm, 4 * n + 3)
                if n:
                    act.wait_ge(v_mm, n)
                act.activation(vT[:], bank[4][:], ACT.Identity, bias=bqkv[:, 2:3]).then_inc(vT_ok, 1)
                act.wait_ge(job_mm, 4 * n + 4)
                if n:
                    act.wait_ge(lg_mm, n)
                act.activation(lgT[:], bank[5][0:NLOG, :], ACT.Copy).then_inc(lgT_ok, 1)

            def post(n):
                act.wait_ge(v_mm, n + 1)
                act.activation(m.v0_h[:, TQ * n:TQ * n + TQ, :], bank[6][:].rearrange("p (t d) -> p t d", t=TQ),
                               ACT.Copy).then_inc(v_hi, 1)

            for s in range(6):
                if s < 4:
                    high_xT(s)
                if 1 <= s <= 4:
                    jobs(s - 1)
                if s >= 2:
                    post(s - 2)

        @block.tensor
        def _(pe):
            pe.wait_ge(const, 9)
            pe.wait_ge(w_in, 16 * W_LOADS)
            for c in range(CH):
                last = pe.transpose(bank[7][:, c * NLOG:(c + 1) * NLOG], wlog[:, c * P:(c + 1) * P], m.ident[0:NLOG, 0:NLOG])
            last.then_inc(wl_mm, 1)

            def turn_x(n):
                for t in range(TQ * n, TQ * n + TQ):
                    pe.wait_ge(xn_ok, t + 1)
                    if t >= 2:
                        pe.wait_ge(xT_lo, t - 1)
                    for c in range(CH):
                        last = pe.transpose(bank[t % 2][:, c * P:(c + 1) * P], xn[:, t, c * P:(c + 1) * P], m.ident[:])
                    last.then_inc(xT_mm, 1)

            def jobs(n):
                cols = slice(512 * n, 512 * n + 512)
                pe.wait_ge(xT_lo, TQ * (n + 1))
                if n == 0:
                    pe.wait_ge(wq_lo, 1)
                    pe.wait_ge(wl_lo, 1)
                for k in range(4):
                    if n:
                        pe.wait_ge((qk_lo, qk_lo, vT_ok, lgT_ok)[k], (2 * n - 1, 2 * n, n, n)[k])
                    wh, wl = (wqkv2_h, wqkv2_l) if k < 3 else (wlogT_h, wlogT_l)
                    out = slice(k * D, k * D + D) if k < 3 else slice(0, P)
                    mm3(pe, bank[2 + k][:], [(wh[:, c, out], wl[:, c, out], xT0_h[:, c, cols], xT0_l[:, c, cols])
                                             for c in range(CH)]).then_inc(job_mm, 1)

            def post(n):
                pe.wait_ge(vT_ok, n + 1)
                if n:
                    pe.wait_ge(v_lo, n)
                for k in range(TQ):
                    last = pe.transpose(bank[6][:, k * D:k * D + D], vT[:, k * P:k * P + P], m.ident[:])
                last.then_inc(v_mm, 1)
                pe.wait_ge(lgT_ok, n + 1)
                if n:
                    pe.wait_ge(lg_ok, TQ * n)
                for k in range(TQ):
                    last = pe.transpose(bank[7][:, k * NLOG:(k + 1) * NLOG], lgT[:, k * P:k * P + P],
                                        m.ident[0:NLOG, 0:NLOG])
                last.then_inc(lg_mm, 1)

            for s in range(6):
                if s < 4:
                    turn_x(s)
                if 1 <= s <= 4:
                    jobs(s - 1)
                if s >= 2:
                    post(s - 2)


def layer0_mix(nc, a, m, bank, bank2):
    with ExitStack() as ctx:
        def sb(name, shape, dt=F32):
            return ctx.enter_context(nc.sbuf_tensor(name, shape, dt))

        def pair(name, shape):
            return sb(name + "_h", shape, F32R), sb(name + "_l", shape, F32R)

        def sem(name):
            return ctx.enter_context(nc.semaphore(name))

        UQ = 4
        UNITS = NT // UQ
        PREP = 2 * KV_HEADS
        PREP_FIRST = 10

        Z, K, T = (sb(n, [P, NT, NS, NS]) for n in ("sk_z", "sk_k", "sk_t"))
        sm, row, col, lrow, lcol, u, v = (sb(n, [P, NT, NS]) for n in ("sk_s", "sk_row", "sk_col", "sk_lr", "sk_lc", "sk_u", "sk_v"))
        rw = sb("rw", [P, NT, 2, NS])
        rws, rwm = sb("rw_s", [P, NT, 2]), sb("rw_m", [P, NT, 2])
        gate = sb("gate", [P, 4])
        xpre = sb("xpre", [P, 4, D])
        xpT_h, xpT_l = pair("xpT", [P, 512])
        y = sb("y", [P, NT, D])
        wbr_h, wbr_l = pair("wbr", [P, D])
        wo0_h, wo0_l = pair("wo0", [P, HID])
        probs = sb("probs0", [P, UQ, S])
        pT_h, pT_l = pair("pT0", [P, 2, 512])
        oT_h, oT_l = pair("oT0", [P, 512])
        nmax, rsum, rinv = sb("nmax0", [P, NT, 2]), sb("rsum0", [P, NT]), sb("rinv0", [P, NT])
        raw = sb("wraw", [P, 2, REP, HID])
        turned = sb("wturned", [P, 2, HID])
        parts_h, parts_l = pair("wparts", [P, 2, 2, HID])
        wbr, wo0 = raw[:, 1, 0, 0:D], raw[:, 1, 1, :]
        xn, x1 = m.xn0, m.acc

        w_in, w_parts, gate_ok = sem("b_w_in"), sem("b_wparts"), sem("b_gate")
        raw_in = [sem(f"b_raw_in{i}") for i in range(2)]
        prep_mm, prep_copy, prep_hi, prep_lo = sem("b_prepmm"), sem("b_prepcopy"), sem("b_prephi"), sem("b_preplo")
        stored = [sem(f"b_stored{i}") for i in range(2)]
        chain, chain_act = sem("b_chain"), sem("b_chainact")
        xp_mm, xp_hi, xp_lo, y_mm, y_ok = (sem("b_" + n) for n in ("xpmm", "xphi", "xplo", "ymm", "y"))
        s_mm, smax, p_exp, p_inv, p_ok = (sem("b_" + n) for n in ("smm", "smax", "pexp", "pinv", "pok"))
        t_mm, t_hi, t_lo, pv_mm = (sem("b_" + n) for n in ("tmm", "thi", "tlo", "pv"))
        o_hi, o_lo, wo_mm, x1_ok, mixed = (sem("b_" + n) for n in ("ohi", "olo", "womm", "x1", "mixed"))

        HEAD_STEPS = 11

        def prep_blocks(unit):
            if unit < 0:
                return range(0, PREP_FIRST)
            per = -(-(PREP - PREP_FIRST) // UNITS)
            return range(min(PREP, PREP_FIRST + per * unit), min(PREP, PREP_FIRST + per * (unit + 1)))

        block = ctx.enter_context(nc.Block())

        @block.sync
        def _(sp):
            sp.dma_start(wbr, a["L0_ffn_W_branch"]).then_inc(w_in, 16)
            sp.dma_start(wo0, a["L0_attn_Wo"]).then_inc(w_in, 16)
            sp.dma_start(gate[:, 0:1], a["L0_ffn_gate"].partition_broadcast(P)).then_inc(w_in, 16)
            for w in range(PREP + 1):
                if w < PREP:
                    g = w // 2
                    if w == 1:
                        sp.wait_ge(w_parts, 4)
                    if w >= 2:
                        sp.wait_ge(prep_mm, REP * (w - 1))
                    src = (a["L1_attn_Wq"][g * REP * D:(g + 1) * REP * D, :] if w % 2 == 0
                           else a["L1_attn_Wo"][:, g * REP * D:(g + 1) * REP * D])
                    sp.dma_start(raw[:, w % 2, :, :], src.rearrange("(r p) c -> p r c", p=P)).then_inc(raw_in[w % 2], 16)
                if w >= 1:
                    for half in range(2):
                        n = 2 * (w - 1) + half
                        g = (w - 1) // 2
                        sp.wait_ge(prep_lo, 2 * n + 2)
                        for k, part in enumerate((parts_h, parts_l)):
                            src = f32(part[:, n % 2, :, :])
                            for r in range(2):
                                h = 2 * half + r
                                dst = (m.wq_s[g, :, k, :, h * D:(h + 1) * D] if (w - 1) % 2 == 0
                                       else m.wo_s[g, :, k, h, :].rearrange("p (c o) -> p c o", c=CH))
                                sp.dma_start(dst, src[:, r, :].rearrange("p (c o) -> p c o", c=CH)).then_inc(stored[n % 2], 16)
            for i in range(2):
                sp.wait_ge(stored[i], PREP * 64)

        @block.gpsimd
        def _(pool):
            pool.wait_ge(w_in, 48)
            pool.tensor_copy(wbr_h[:], wbr).then_inc(w_parts, 1)
            pool.tensor_copy(wo0_h[:], wo0).then_inc(w_parts, 1)
            pool.wait_ge(w_parts, 2)
            pool.tensor_tensor(wbr_l[:], wbr, f32(wbr_h[:]), ALU.subtract).then_inc(w_parts, 1)
            pool.tensor_tensor(wo0_l[:], wo0, f32(wo0_h[:]), ALU.subtract).then_inc(w_parts, 1)

            def prep(unit):
                for w in prep_blocks(unit):
                    for r in range(REP):
                        n = w * REP + r
                        half = n // 2
                        pool.wait_ge(prep_hi, n + 1)
                        if half >= 2:
                            pool.wait_ge(stored[half % 2], 64 * (half // 2))
                        pool.tensor_tensor(parts_l[:, half % 2, r % 2, :], turned[:, n % 2, :],
                                           f32(parts_h[:, half % 2, r % 2, :]), ALU.subtract).then_inc(prep_lo, 1)

            prep(-1)
            for unit in range(UNITS):
                for qt in range(UQ):
                    t = UQ * unit + qt
                    pool.wait_ge(p_inv, t + 1)
                    pool.tensor_scalar(probs[:, qt, :], probs[:, qt, :], rinv[:, t:t + 1], 1.0, ALU.mult,
                                       ALU.mult).then_inc(p_ok, 1)
                prep(unit)

        @block.vector
        def _(dve):
            done = [0, 0]

            def after(ins):
                done[0] += 1
                ins.then_inc(chain, 1)
                dve.wait_ge(chain, done[0])

            def after_act():
                done[1] += 1
                dve.wait_ge(chain_act, done[1])

            rows = lambda x: x[:]
            cols = lambda x: x[:].rearrange("p t i j -> p t j i")
            over_rows = lambda x: x[:].unsqueeze(3).to_broadcast([P, NT, NS, NS])
            over_cols = lambda x: x[:].unsqueeze(2).to_broadcast([P, NT, NS, NS])

            pq = m.logits[:, :, NZ:NLOG].rearrange("p t (k n) -> p t k n", k=2)
            wide = lambda x: x[:].unsqueeze(3).to_broadcast([P, NT, 2, NS])
            after(dve.tensor_reduce(rwm[:], pq, AX.X, ALU.max))
            after(dve.tensor_tensor(rw[:], pq, wide(rwm), ALU.subtract))
            after_act()
            after(dve.tensor_reduce(rws[:], rw[:], AX.X, ALU.add))
            after(dve.reciprocal(rwm[:], rws[:]))
            after(dve.tensor_tensor(rw[:], rw[:], wide(rwm), ALU.mult))
            dve.wait_ge(gate_ok, 1)
            after(dve.tensor_scalar(gate[:, 1:2], gate[:, 1:2], 1.0, None, ALU.add))
            after(dve.reciprocal(gate[:, 2:3], gate[:, 1:2]))
            after(dve.tensor_scalar(gate[:, 3:4], gate[:, 2:3], -1.0, 1.0, ALU.mult, ALU.add))
            after(dve.tensor_scalar(Z[:], m.logits[:, :, 0:NZ].rearrange("p t (i j) -> p t i j", i=NS), 1.0 / TAU, None, ALU.mult))
            after(dve.tensor_reduce(u[:], rows(Z), AX.X, ALU.max))
            after(dve.tensor_tensor(T[:], Z[:], over_rows(u), ALU.subtract))
            assert done[0] == HEAD_STEPS

            for n in range(4):
                for k in range(4):
                    t = 4 * n + k
                    if n:
                        dve.wait_ge(xp_mm, n)
                    after(dve.tensor_scalar(xpre[:, k, :], xn[:, t, 0:D], rw[:, t, 0, 0:1], None, ALU.mult))
                    for j in range(1, NS):
                        last = dve.scalar_tensor_tensor(out=xpre[:, k, :], in0=xn[:, t, j * D:(j + 1) * D],
                                                        scalar=rw[:, t, 0, j:j + 1], in1=xpre[:, k, :],
                                                        op0=ALU.mult, op1=ALU.add)
                        after(last)
                dve.wait_ge(xp_hi, n + 1)
                dve.tensor_tensor(xpT_l[:], bank[6][:], f32(xpT_h[:]), ALU.subtract).then_inc(xp_lo, 1)

            after_act()
            after(dve.tensor_reduce(sm[:], rows(T), AX.X, ALU.add))
            after_act()
            after(dve.tensor_tensor(u[:], u[:], lrow[:], ALU.add))
            after(dve.tensor_tensor(Z[:], Z[:], over_rows(u), ALU.subtract))
            after(dve.tensor_reduce(v[:], cols(Z), AX.X, ALU.max))
            after(dve.tensor_tensor(T[:], Z[:], over_cols(v), ALU.subtract))
            after_act()
            after(dve.tensor_reduce(sm[:], cols(T), AX.X, ALU.add))
            after_act()
            after(dve.tensor_tensor(v[:], v[:], lcol[:], ALU.add))
            after(dve.tensor_tensor(Z[:], Z[:], over_cols(v), ALU.subtract))
            after_act()
            steps = SINKHORN_ITERS - 1
            for part, count in enumerate((steps - SINKHORN_CHUNK, SINKHORN_CHUNK)):
                if part:
                    after_act()
                    after_act()
                    after(dve.tensor_tensor(Z[:], Z[:], over_rows(lrow), ALU.add))
                    after(dve.tensor_tensor(Z[:], Z[:], over_cols(lcol), ALU.add))
                    after_act()
                after(dve.memset(col[:], 1.0))
                base = done[0]
                with dve.Fori(0, count) as it:
                    dve.wait_ge(chain, it * 6 + base)
                    dve.tensor_tensor(T[:], K[:], over_cols(col), ALU.mult).then_inc(chain, 1)
                    dve.wait_ge(chain, it * 6 + (base + 1))
                    dve.tensor_reduce(sm[:], rows(T), AX.X, ALU.add).then_inc(chain, 1)
                    dve.wait_ge(chain, it * 6 + (base + 2))
                    dve.reciprocal(row[:], sm[:]).then_inc(chain, 1)
                    dve.wait_ge(chain, it * 6 + (base + 3))
                    dve.tensor_tensor(T[:], K[:], over_rows(row), ALU.mult).then_inc(chain, 1)
                    dve.wait_ge(chain, it * 6 + (base + 4))
                    dve.tensor_reduce(sm[:], cols(T), AX.X, ALU.add).then_inc(chain, 1)
                    dve.wait_ge(chain, it * 6 + (base + 5))
                    dve.reciprocal(col[:], sm[:]).then_inc(chain, 1)
                done[0] = base + 6 * count
                dve.wait_ge(chain, done[0])
            after(dve.tensor_tensor(T[:], K[:], over_rows(row), ALU.mult))
            after(dve.tensor_tensor(T[:], T[:], over_cols(col), ALU.mult))
            mix = T[:].rearrange("p t i j -> p t (i j)")
            after(dve.tensor_scalar(mix, mix, gate[:, 2:3], None, ALU.mult))
            after(dve.tensor_scalar(mix[:, :, 0:NZ:NS + 1], mix[:, :, 0:NZ:NS + 1], gate[:, 3:4], None, ALU.add))

            mixes = [0]

            def mix_tile(t):
                if t == 0:
                    dve.wait_ge(y_ok, 4)
                for j in range(NS + 1):
                    for i in range(NS):
                        cols = slice(i * D, i * D + D)
                        if j:
                            dve.wait_ge(mixed, mixes[0] - NS + 1)
                        dve.scalar_tensor_tensor(
                            out=x1[:, t, cols], in0=xn[:, t, j * D:(j + 1) * D] if j < NS else y[:, t, :],
                            scalar=T[:, t, i, j:j + 1] if j < NS else rw[:, t, 1, i:i + 1], in1=x1[:, t, cols],
                            op0=ALU.mult, op1=ALU.add).then_inc(mixed, 1)
                        mixes[0] += 1

            for unit in range(UNITS):
                for qt in range(UQ):
                    t = UQ * unit + qt
                    dve.wait_ge(s_mm, t + 1)
                    view = bank2[2 + 2 * (t % 2)]
                    dve.tensor_reduce(nmax[:, t, 0:1], view, AX.X, ALU.max, negate=True).then_inc(smax, 1)
                    dve.wait_ge(smax, 2 * t + 1)
                    dve.tensor_scalar(nmax[:, t, 1:2], nmax[:, t, 0:1], SCALE, None, ALU.mult).then_inc(smax, 1)
                    mix_tile(t)
                    dve.wait_ge(p_exp, t + 1)
                    dve.reciprocal(rinv[:, t:t + 1], rsum[:, t:t + 1]).then_inc(p_inv, 1)
                for j in range(TB):
                    n = TB * unit + j
                    dve.wait_ge(t_hi, n + 1)
                    dve.tensor_tensor(pT_l[:, n % 2, :], bank[n % 2][:], f32(pT_h[:, n % 2, :]), ALU.subtract).then_inc(t_lo, 1)
                dve.wait_ge(o_hi, unit + 1)
                dve.tensor_tensor(oT_l[:], bank[6][:], f32(oT_h[:]), ALU.subtract).then_inc(o_lo, 1)
                for qt in range(UQ):
                    t = UQ * unit + qt
                    dve.wait_ge(wo_mm, t + 1)
                    dve.wait_ge(mixed, NS * (NS + 1) * (t + 1))
                    dve.tensor_tensor(x1[:, t, :], x1[:, t, :], bank[7][:], ALU.add).then_inc(x1_ok, 1)

        @block.scalar
        def _(act):
            done = [0, 0]

            def chain_step(at, out, in_, func):
                act.wait_ge(chain, at)
                act.activation(out, in_, func).then_inc(chain_act, 1)

            chain_step(2, rw[:], rw[:], ACT.Exp)
            act.wait_ge(w_in, 48)
            act.activation(gate[:, 1:2], gate[:, 0:1], ACT.Exp, scale=-1.0).then_inc(gate_ok, 1)
            at = HEAD_STEPS
            chain_step(at, T[:], T[:], ACT.Exp)
            for n in range(4):
                act.wait_ge(xp_mm, n + 1)
                if n:
                    act.wait_ge(y_mm, n)
                act.activation(xpT_h[:], bank[6][:], ACT.Copy).then_inc(xp_hi, 1)
                act.wait_ge(y_mm, n + 1)
                act.activation(y[:, 4 * n:4 * n + 4, :], bank[7][:].rearrange("p (t d) -> p t d", t=4), ACT.Copy).then_inc(y_ok, 1)
            at += NT * NS + 1
            chain_step(at, lrow[:], sm[:], ACT.Ln)
            chain_step(at + 4, T[:], T[:], ACT.Exp)
            chain_step(at + 5, lcol[:], sm[:], ACT.Ln)
            chain_step(at + 7, K[:], Z[:], ACT.Exp)
            at += 8 + 6 * (SINKHORN_ITERS - 1 - SINKHORN_CHUNK)

            def prep(blocks):
                for w in blocks:
                    for r in range(REP):
                        n = w * REP + r
                        half = n // 2
                        act.wait_ge(prep_mm, n + 1)
                        if n >= 2:
                            act.wait_ge(prep_lo, n - 1)
                        act.activation(turned[:, n % 2, :], bank[n % 2][:], ACT.Copy).then_inc(prep_copy, 1)
                        if half >= 2:
                            act.wait_ge(stored[half % 2], 64 * (half // 2))
                        act.activation(parts_h[:, half % 2, r % 2, :], bank[n % 2][:], ACT.Copy).then_inc(prep_hi, 1)

            prep(range(0, 5))
            chain_step(at, lrow[:], row[:], ACT.Ln)
            chain_step(at, lcol[:], col[:], ACT.Ln)
            chain_step(at + 2, K[:], Z[:], ACT.Exp)
            prep(range(5, PREP_FIRST))
            for unit in range(UNITS):
                for qt in range(UQ):
                    t = UQ * unit + qt
                    act.wait_ge(smax, 2 * t + 2)
                    if unit:
                        act.wait_ge(t_mm, TB * unit)
                    act.activation(probs[:, qt, :], bank2[2 + 2 * (t % 2)], ACT.Exp, bias=nmax[:, t, 1:2],
                                   scale=SCALE, accum_out=rsum[:, t:t + 1]).then_inc(p_exp, 1)
                for j in range(TB):
                    n = TB * unit + j
                    act.wait_ge(t_mm, n + 1)
                    if n >= 2:
                        act.wait_ge(pv_mm, n - 1)
                    act.activation(pT_h[:, n % 2, :], bank[n % 2][:], ACT.Copy).then_inc(t_hi, 1)
                act.wait_ge(pv_mm, TB * (unit + 1))
                if unit:
                    act.wait_ge(wo_mm, UQ * unit)
                act.activation(oT_h[:], bank[6][:], ACT.Copy).then_inc(o_hi, 1)
                prep(prep_blocks(unit))

        @block.tensor
        def _(pe):
            for n in range(4):
                pe.wait_ge(chain, HEAD_STEPS + 4 * NS * (n + 1))
                if n:
                    pe.wait_ge(xp_lo, n)
                for k in range(4):
                    last = pe.transpose(bank[6][:, k * P:(k + 1) * P], xpre[:, k, :], m.ident[:])
                last.then_inc(xp_mm, 1)
                pe.wait_ge(xp_lo, n + 1)
                pe.wait_ge(w_parts, 4)
                if n:
                    pe.wait_ge(y_ok, n)
                for k in range(4):
                    cols = slice(k * P, (k + 1) * P)
                    last = mm3(pe, bank[7][:, cols], [(xpT_h[:, cols], xpT_l[:, cols], wbr_h[:], wbr_l[:])])
                last.then_inc(y_mm, 1)

            def prep(unit):
                for w in prep_blocks(unit):
                    pe.wait_ge(raw_in[w % 2], 16 * (w // 2 + 1))
                    for r in range(REP):
                        n = w * REP + r
                        if n >= 2:
                            pe.wait_ge(prep_hi, n - 1)
                        if unit >= 0:
                            pe.wait_ge(t_lo, TB * (unit + 1))
                        for c in range(CH):
                            src = raw[:, w % 2, r, c * P:(c + 1) * P] if w % 2 == 0 else raw[:, w % 2, c, r * D:(r + 1) * D]
                            last = pe.transpose(bank[n % 2][:, c * P:(c + 1) * P], src, m.ident[:])
                        last.then_inc(prep_mm, 1)

            prep(-1)
            for unit in range(UNITS):
                b = unit * UQ // TB
                for qt in range(UQ):
                    t = UQ * unit + qt
                    if t >= 2:
                        pe.wait_ge(p_exp, t - 1)
                    qs = slice(t * P, t * P + P)
                    for half in range(2):
                        ks = slice(b * S + 512 * half, b * S + 512 * half + 512)
                        last = mm3(pe, bank[2 + 2 * (t % 2) + half][:], [(m.q0_h[:, qs], m.q0_l[:, qs], m.k0_h[:, ks], m.k0_l[:, ks])])
                    last.then_inc(s_mm, 1)
                pe.wait_ge(p_ok, UQ * (unit + 1))
                pe.wait_ge(prep_hi, REP * (prep_blocks(unit - 1).stop))

                def weigh(j):
                    n = TB * unit + j
                    pe.wait_ge(t_lo, n + 1)
                    vh, vl = m.v0_h[:, b * TB + j, :], m.v0_l[:, b * TB + j, :]
                    mm3(pe, bank[6][:], [(vh, vl, pT_h[:, n % 2, :], pT_l[:, n % 2, :])], start=j == 0,
                        stop=j == TB - 1).then_inc(pv_mm, 1)

                if unit:
                    pe.wait_ge(o_lo, unit)
                for j in range(TB):
                    n = TB * unit + j
                    if n >= 2:
                        pe.wait_ge(t_lo, n - 1)
                    for qt in range(UQ):
                        last = pe.transpose(bank[n % 2][:, qt * P:(qt + 1) * P], probs[:, qt, j * P:(j + 1) * P], m.ident[:])
                    last.then_inc(t_mm, 1)
                    if j:
                        weigh(j - 1)
                weigh(TB - 1)
                for qt in range(UQ):
                    t = UQ * unit + qt
                    pe.wait_ge(o_lo, unit + 1)
                    if t:
                        pe.wait_ge(x1_ok, t)
                    qs = slice(qt * P, qt * P + P)
                    mm3(pe, bank[7][:], [(oT_h[:, qs], oT_l[:, qs], wo0_h[:], wo0_l[:])]).then_inc(wo_mm, 1)
                prep(unit)


def layer1_ffn(nc, a, m, bank):
    with ExitStack() as ctx:
        def sb(name, shape, dt=F32):
            return ctx.enter_context(nc.sbuf_tensor(name, shape, dt))

        def pair(name, shape):
            return sb(name + "_h", shape, F32R), sb(name + "_l", shape, F32R)

        def sem(name):
            return ctx.enter_context(nc.semaphore(name))

        TQ = 4
        xn, x1 = sb("xn1", [P, NT, HID]), m.acc
        wf_raw = sb("wf_raw", [P, CH, HID])
        wf_h, wf_l = pair("wf", [P, CH, HID])
        gw1_raw = sb("gw1_raw", [GH, HID])
        gw1_h, gw1_l = pair("gw1", [P, CH, P])
        la_raw = sb("la_raw", [P, CH, EXP, RANK])
        la_h, la_l = pair("la", [P, CH, P])
        lb_raw = sb("lb_raw", [P, HID])
        lb_h, lb_l = pair("lb", [P, HID])
        gb1 = sb("gb1", [GH, 1])
        gamma, beta = sb("gamma", [P, GH]), sb("beta", [P, GH])
        gw2, gb2 = sb("gw2", [P, EXP, GH]), sb("gb2", [P, EXP])
        st, mv = sb("st1", [P, NT, 6]), sb("mv1", [P, NT, 2])
        veps, rstd, mhalf = sb("veps1", [P, NT]), sb("rstd1", [P, NT]), sb("mhalf1", [P, NT])
        tmpT = sb("tmpT", [P, N])
        hT = sb("hT", [GH, 512])
        h, hs = sb("h", [P, NT, GH]), sb("hs", [P, NT, GH])
        hstat = sb("hstat", [P, 3, NT])
        gates, score, rev = sb("gates", [P, NT, EXP]), sb("score", [P, NT, EXP]), sb("rev", [P, NT, EXP])
        pick = sb("pick", [P, NT, TOPK, EXP])
        top, best = sb("top", [P, TOPK, NT]), sb("best", [P, NT])
        tg = sb("tg", [P, TOPK, NT])
        counts, allowed = sb("counts", [P, TOPK * EXP]), sb("allowed", [P, TOPK, EXP])
        w = sb("w", [P, NT, EXP])
        wexp = sb("wexp", [P, TQ, EXP, RANK])
        tw = sb("tw", [P, 512])
        tw_h, tw_l = pair("twp", [P, 512])

        w_in, const, w_hi, w_lo = sem("c_w_in"), sem("c_const"), sem("c_whi"), sem("c_wlo")
        wt_mm, wt_hi, wt_lo = sem("c_wtmm"), sem("c_wthi"), sem("c_wtlo")
        st_done, mv_done, var_eps, rstd_ok, xn_ok = sem("c_st"), sem("c_mv"), sem("c_var"), sem("c_rstd"), sem("c_xn")
        xT_mm, xT_hi, xT_lo = sem("c_xTmm"), sem("c_xThi"), sem("c_xTlo")
        h_mm, hT_ok, ht_mm, h_ok, lr_mm, lr_ok = (sem("c_" + n) for n in ("hmm", "hT", "htmm", "h", "lrmm", "lr"))
        main_mm, main_ok = sem("c_main"), sem("c_mainok")
        chain, hvar, hrstd, diff, ediff, cnt_mm = (sem("c_" + n) for n in ("chain", "hvar", "hrstd", "diff", "ediff", "cnt"))
        wx_ok, wx_mm, tw_ok, tw_hi, tw_lo, lora_mm, lora_ok = (
            sem("c_" + n) for n in ("wx", "wxmm", "tw", "twhi", "twlo", "lora", "loraok"))
        spilled = sem("c_spilled")
        W_LOADS = 8 + CH

        block = ctx.enter_context(nc.Block())

        @block.sync
        def _(sp):
            loads = [(wf_raw[:], a["L1_ffn_weight"].rearrange("(r p) i -> p r i", p=P)), (gw1_raw[:], a["L1_ffn_gw1"]),
                     (lb_raw[:], a["L1_ffn_lora_B"].rearrange("e r o -> (e r) o")),
                     (gb1[:], a["L1_ffn_gb1"].rearrange("(g o) -> g o", o=1)),
                     (gamma[:], a["L1_ffn_ln_gamma"].partition_broadcast(P)),
                     (beta[:], a["L1_ffn_ln_beta"].partition_broadcast(P)),
                     (gw2[:].rearrange("p e g -> p (e g)"), a["L1_ffn_gw2"].rearrange("e g -> (e g)").partition_broadcast(P)),
                     (gb2[:], a["L1_ffn_gb2"].partition_broadcast(P))]
            loads += [(la_raw[:, c, :, :], a["L1_ffn_lora_A"][:, c * P:(c + 1) * P, :].rearrange("e p r -> p e r"))
                      for c in range(CH)]
            for dst, src in loads:
                sp.dma_start(dst, src).then_inc(w_in, 16)
            for b in range(B):
                sp.wait_ge(xT_lo, TB * (b + 1))
                for k, part in enumerate((m.xT_h, m.xT_l)):
                    sp.dma_start(m.xT_s[b, :, k, :, :], f32(part[:, :, b * S:(b + 1) * S])).then_inc(spilled, 16)
            sp.wait_ge(spilled, 16 * 2 * B)

        @block.gpsimd
        def _(pool):
            pool.memset(mhalf[:], -0.5).then_inc(const, 1)
            pool.memset(f32(gw1_h[:]), 0.0).then_inc(const, 1)
            pool.memset(f32(gw1_l[:]), 0.0).then_inc(const, 1)
            for e in range(EXP):
                pool.memset(rev[:, :, e:e + 1], float(EXP - e)).then_inc(const, 1)
            pool.wait_ge(const, 3 + EXP)
            for n in range(4):
                cols = slice(TQ * n, TQ * n + TQ)
                pool.wait_ge(mv_done, TQ * (n + 1))
                pool.tensor_scalar(veps[:, cols], mv[:, cols, 1], 1.0, LN_EPS, ALU.mult, ALU.add).then_inc(var_eps, 1)
                pool.wait_ge(var_eps, n + 1)
                pool.tensor_tensor(rstd[:, cols], veps[:, cols], mhalf[:, cols], ALU.pow).then_inc(rstd_ok, 1)
                if n == 0:
                    pool.wait_ge(w_hi, 2)
                    pool.tensor_tensor(la_l[:], la_raw[:].rearrange("p c e r -> p c (e r)"), f32(la_h[:]), ALU.subtract).then_inc(w_lo, 1)
                    pool.tensor_tensor(lb_l[:], lb_raw[:], f32(lb_h[:]), ALU.subtract).then_inc(w_lo, 1)
            pool.wait_ge(hvar, 1)
            pool.tensor_tensor(hstat[:, 2, :], hstat[:, 1, :], mhalf[:], ALU.pow).then_inc(hrstd, 1)

        @block.vector
        def _(dve):
            steps = [0]

            def after(ins):
                steps[0] += 1
                ins.then_inc(chain, 1)
                dve.wait_ge(chain, steps[0])

            def stats(n):
                for t in range(TQ * n, TQ * n + TQ):
                    dve.bn_stats(st[:, t, :], x1[:, t, :]).then_inc(st_done, 1)
                for t in range(TQ * n, TQ * n + TQ):
                    dve.wait_ge(st_done, t + 1)
                    dve.bn_aggr(mv[:, t, :], st[:, t, :]).then_inc(mv_done, 1)

            def norm(n):
                dve.wait_ge(rstd_ok, n + 1)
                dve.wait_ge(mv_done, TQ * n + TQ)
                for t in range(TQ * n, TQ * n + TQ):
                    dve.tensor_scalar(xn[:, t, :], x1[:, t, :], mv[:, t, 0:1], rstd[:, t:t + 1], ALU.subtract,
                                      ALU.mult).then_inc(xn_ok, 1)

            def low_xT(n):
                for t in range(TQ * n, TQ * n + TQ):
                    dve.wait_ge(xT_hi, t + 1)
                    cols = slice(t * P, t * P + P)
                    dve.tensor_tensor(m.xT_l[:, :, cols], bank[t % 2][:].rearrange("p (c t) -> p c t", c=CH),
                                      f32(m.xT_h[:, :, cols]), ALU.subtract).then_inc(xT_lo, 1)

            def add_main(n):
                for t in range(TQ * n, TQ * n + TQ):
                    dve.wait_ge(main_mm, t + 1)
                    dve.wait_ge(xn_ok, t + 1)
                    dve.tensor_tensor(x1[:, t, :], x1[:, t, :], bank[4 + t % 2][:], ALU.add).then_inc(main_ok, 1)

            def hidden(n):
                dve.wait_ge(ht_mm, n + 1)
                dve.tensor_copy(h[:, TQ * n:TQ * n + TQ, :], bank[7][:, 0:TQ * GH].rearrange("p (t g) -> p t g", t=TQ)).then_inc(h_ok, 1)

            stats(0)
            for n in range(4):
                if n < 3:
                    stats(n + 1)
                norm(n)
                if n == 0:
                    dve.wait_ge(wt_hi, 1)
                    dve.tensor_tensor(gw1_l[:, :, 0:GH], bank[7][:, 0:CH * GH].rearrange("p (c g) -> p c g", c=CH),
                                      f32(gw1_h[:, :, 0:GH]), ALU.subtract).then_inc(wt_lo, 1)
                    for r in range(CH):
                        dve.wait_ge(wt_hi, r + 2)
                        cols = slice(r * P, r * P + P)
                        dve.tensor_tensor(wf_l[:, :, cols], bank[4 + r % 2][:].rearrange("p (c o) -> p c o", c=CH),
                                          f32(wf_h[:, :, cols]), ALU.subtract).then_inc(wt_lo, 1)
                low_xT(n)
                if n:
                    hidden(n - 1)
                    add_main(n - 1)
            hidden(3)
            wide = lambda x: x.unsqueeze(2).to_broadcast([P, NT, GH])
            along = lambda x: x[:].unsqueeze(1).to_broadcast([P, NT, GH])
            dve.wait_ge(h_ok, 4)
            after(dve.tensor_reduce(hstat[:, 0, :], h[:], AX.X, ALU.add))
            after(dve.tensor_scalar(hstat[:, 0, :], hstat[:, 0, :], 1.0 / GH, None, ALU.mult))
            after(dve.tensor_tensor(h[:], h[:], wide(hstat[:, 0, :]), ALU.subtract))
            after(dve.tensor_tensor(hs[:], h[:], h[:], ALU.mult))
            after(dve.tensor_reduce(hstat[:, 1, :], hs[:], AX.X, ALU.add))
            dve.tensor_scalar(hstat[:, 1, :], hstat[:, 1, :], 1.0 / GH, LN_EPS, ALU.mult, ALU.add).then_inc(hvar, 1)
            add_main(3)
            dve.wait_ge(hrstd, 1)
            after(dve.tensor_tensor(h[:], h[:], wide(hstat[:, 2, :]), ALU.mult))
            after(dve.tensor_tensor(h[:], h[:], along(gamma), ALU.mult))
            after(dve.tensor_tensor(h[:], h[:], along(beta), ALU.add))
            after(dve.tensor_scalar(h[:], h[:], 0.0, None, ALU.max))
            for e in range(EXP):
                after(dve.tensor_tensor(hs[:], h[:], gw2[:, e, :].unsqueeze(1).to_broadcast([P, NT, GH]), ALU.mult))
                after(dve.tensor_reduce(gates[:, :, e], hs[:], AX.X, ALU.add))
            after(dve.tensor_tensor(gates[:], gates[:], gb2[:].unsqueeze(1).to_broadcast([P, NT, EXP]), ALU.add))
            bc = lambda x: x.unsqueeze(2).to_broadcast([P, NT, EXP])
            for k in range(TOPK):
                after(dve.tensor_reduce(top[:, k, :], gates[:], AX.X, ALU.max))
                after(dve.tensor_tensor(score[:], gates[:], bc(top[:, k, :]), ALU.is_ge))
                after(dve.tensor_tensor(score[:], score[:], rev[:], ALU.mult))
                after(dve.tensor_reduce(best[:], score[:], AX.X, ALU.max))
                after(dve.tensor_tensor(pick[:, :, k, :], score[:], bc(best[:]), ALU.is_equal))
                if k + 1 < TOPK:
                    after(dve.scalar_tensor_tensor(out=gates[:], in0=pick[:, :, k, :], scalar=-1e38, in1=gates[:],
                                                   op0=ALU.mult, op1=ALU.add))
            dve.tensor_tensor(best[:], top[:, 1, :], top[:, 0, :], ALU.subtract).then_inc(diff, 1)
            dve.tensor_reduce(counts[:], pick[:].rearrange("p t k e -> p (k e) t"), AX.X, ALU.add).then_inc(diff, 1)
            dve.wait_ge(ediff, 1)
            after(dve.tensor_scalar(tg[:, 0, :], tg[:, 1, :], 1.0, None, ALU.add))
            after(dve.reciprocal(tg[:, 0, :], tg[:, 0, :]))
            after(dve.tensor_tensor(tg[:, 1, :], tg[:, 1, :], tg[:, 0, :], ALU.mult))
            dve.wait_ge(cnt_mm, 1)
            after(dve.tensor_scalar(allowed[:].rearrange("p k e -> p (k e)"), bank[6][:, 0:TOPK * EXP], float(CAPACITY), ALPHA,
                                    ALU.is_le, ALU.mult))
            for k in range(TOPK):
                after(dve.tensor_tensor(pick[:, :, k, :], pick[:, :, k, :], bc(tg[:, k, :]), ALU.mult))
                after(dve.tensor_tensor(pick[:, :, k, :], pick[:, :, k, :],
                                        allowed[:, k, :].unsqueeze(1).to_broadcast([P, NT, EXP]), ALU.mult))
            after(dve.tensor_tensor(w[:], pick[:, :, 0, :], pick[:, :, 1, :], ALU.add))
            for n in range(4):
                if n:
                    dve.wait_ge(wx_mm, n)
                dve.tensor_copy(wexp[:], w[:, TQ * n:TQ * n + TQ, :].unsqueeze(3).to_broadcast([P, TQ, EXP, RANK])).then_inc(wx_ok, 1)
                dve.wait_ge(wx_mm, n + 1)
                if n == 0:
                    dve.wait_ge(lr_ok, 4)
                if n:
                    dve.wait_ge(tw_lo, n)
                dve.tensor_tensor(tw[:], tmpT[:, 512 * n:512 * n + 512], bank[0][:], ALU.mult).then_inc(tw_ok, 1)
                dve.wait_ge(tw_hi, n + 1)
                dve.tensor_tensor(tw_l[:], tw[:], f32(tw_h[:]), ALU.subtract).then_inc(tw_lo, 1)
                for t in range(TQ * n, TQ * n + TQ):
                    dve.wait_ge(lora_mm, t + 1)
                    if t == 0:
                        dve.wait_ge(main_ok, NT)
                    dve.tensor_tensor(x1[:, t, :], x1[:, t, :], bank[4 + t % 2][:], ALU.add).then_inc(lora_ok, 1)

        @block.scalar
        def _(act):
            act.wait_ge(const, 3 + EXP)
            act.wait_ge(wt_mm, 1)
            act.activation(gw1_h[:, :, 0:GH], bank[7][:, 0:CH * GH].rearrange("p (c g) -> p c g", c=CH), ACT.Copy).then_inc(wt_hi, 1)
            for r in range(CH):
                act.wait_ge(wt_mm, r + 2)
                act.activation(wf_h[:, :, r * P:(r + 1) * P], bank[4 + r % 2][:].rearrange("p (c o) -> p c o", c=CH),
                               ACT.Copy).then_inc(wt_hi, 1)
            act.wait_ge(w_in, 16 * W_LOADS)
            act.activation(la_h[:], la_raw[:].rearrange("p c e r -> p c (e r)"), ACT.Copy).then_inc(w_hi, 1)
            act.activation(lb_h[:], lb_raw[:], ACT.Copy).then_inc(w_hi, 1)
            for n in range(5):
                if n < 4:
                    for t in range(TQ * n, TQ * n + TQ):
                        act.wait_ge(xT_mm, t + 1)
                        act.activation(m.xT_h[:, :, t * P:t * P + P], bank[t % 2][:].rearrange("p (c t) -> p c t", c=CH),
                                       ACT.Copy).then_inc(xT_hi, 1)
                if n:
                    act.wait_ge(h_mm, n)
                    if n > 1:
                        act.wait_ge(ht_mm, n - 1)
                    act.activation(hT[:], bank[2][0:GH, :], ACT.Identity, bias=gb1[:]).then_inc(hT_ok, 1)
                    act.wait_ge(lr_mm, n)
                    act.activation(tmpT[:, 512 * (n - 1):512 * n], bank[3][:], ACT.Copy).then_inc(lr_ok, 1)
            act.wait_ge(diff, 1)
            act.activation(tg[:, 1, :], best[:], ACT.Exp).then_inc(ediff, 1)
            for n in range(4):
                act.wait_ge(tw_ok, n + 1)
                if n:
                    act.wait_ge(lora_mm, TQ * n)
                act.activation(tw_h[:], tw[:], ACT.Copy).then_inc(tw_hi, 1)

        @block.tensor
        def _(pe):
            pe.wait_ge(w_in, 16 * W_LOADS)
            for c in range(CH):
                last = pe.transpose(bank[7][:, c * GH:(c + 1) * GH], gw1_raw[:, c * P:(c + 1) * P], m.ident[0:GH, 0:GH])
            last.then_inc(wt_mm, 1)
            for r in range(CH):
                if r >= 2:
                    pe.wait_ge(wt_lo, r)
                for c in range(CH):
                    last = pe.transpose(bank[4 + r % 2][:, c * P:(c + 1) * P], wf_raw[:, r, c * P:(c + 1) * P], m.ident[:])
                last.then_inc(wt_mm, 1)

            def turn_x(n):
                for t in range(TQ * n, TQ * n + TQ):
                    pe.wait_ge(xn_ok, t + 1)
                    if t >= 2:
                        pe.wait_ge(xT_lo, t - 1)
                    for c in range(CH):
                        last = pe.transpose(bank[t % 2][:, c * P:(c + 1) * P], xn[:, t, c * P:(c + 1) * P], m.ident[:])
                    last.then_inc(xT_mm, 1)

            def products(n):
                cols = slice(512 * n, 512 * n + 512)
                pe.wait_ge(xT_lo, TQ * (n + 1))
                if n == 0:
                    pe.wait_ge(wt_lo, 1 + CH)
                    pe.wait_ge(w_lo, 2)
                if n:
                    pe.wait_ge(hT_ok, n)
                mm3(pe, bank[2][:], [(gw1_h[:, c, :], gw1_l[:, c, :], m.xT_h[:, c, cols], m.xT_l[:, c, cols])
                                     for c in range(CH)]).then_inc(h_mm, 1)
                if n:
                    pe.wait_ge(lr_ok, n)
                mm3(pe, bank[3][:], [(la_h[:, c, :], la_l[:, c, :], m.xT_h[:, c, cols], m.xT_l[:, c, cols])
                                     for c in range(CH)]).then_inc(lr_mm, 1)
                pe.wait_ge(hT_ok, n + 1)
                if n:
                    pe.wait_ge(h_ok, n)
                for k in range(TQ):
                    last = pe.transpose(bank[7][:, k * GH:(k + 1) * GH], hT[:, k * P:(k + 1) * P], m.ident[0:GH, 0:GH])
                last.then_inc(ht_mm, 1)
                for t in range(TQ * n, TQ * n + TQ):
                    if t >= 2:
                        pe.wait_ge(main_ok, t - 1)
                    ts = slice(t * P, t * P + P)
                    mm3(pe, bank[4 + t % 2][:], [(m.xT_h[:, c, ts], m.xT_l[:, c, ts], wf_h[:, c, :], wf_l[:, c, :])
                                                 for c in range(CH)]).then_inc(main_mm, 1)

            turn_x(0)
            for n in range(4):
                if n < 3:
                    turn_x(n + 1)
                products(n)
            pe.wait_ge(diff, 2)
            pe.matmul(bank[6][:, 0:TOPK * EXP], m.ones[:], counts[:], start=True, stop=True).then_inc(cnt_mm, 1)
            for n in range(4):
                pe.wait_ge(wx_ok, n + 1)
                if n:
                    pe.wait_ge(tw_ok, n)
                for k in range(TQ):
                    last = pe.transpose(bank[0][:, k * P:(k + 1) * P], wexp[:, k, :, :].rearrange("p e r -> p (e r)"), m.ident[:])
                last.then_inc(wx_mm, 1)
                pe.wait_ge(tw_lo, n + 1)
                for t in range(TQ * n, TQ * n + TQ):
                    k = t % TQ
                    pe.wait_ge(main_ok, NT) if t < 2 else pe.wait_ge(lora_ok, t - 1)
                    ts = slice(k * P, k * P + P)
                    mm3(pe, bank[4 + t % 2][:], [(tw_h[:, ts], tw_l[:, ts], lb_h[:], lb_l[:])]).then_inc(lora_mm, 1)


def layer1_keys(nc, a, m, bank):
    with ExitStack() as ctx:
        def sb(name, shape, dt=F32):
            return ctx.enter_context(nc.sbuf_tensor(name, shape, dt))

        def pair(name, shape):
            return sb(name + "_h", shape, F32R), sb(name + "_l", shape, F32R)

        def sem(name):
            return ctx.enter_context(nc.semaphore(name))

        RAWW = 1024
        dn_h, dn_l = pair("dn", [P, CH, KV_HEADS, 2, LAT])
        up_h, up_l = pair("up", [P, 2, LC, KVW])
        cmp_h, cmp_l = pair("cmp", [P, 2 * LC, S])
        raw = sb("kv_raw", [P, 2, RAWW])
        SLOTS = 3
        st_h, st_l = pair("kv_out", [P, SLOTS, 512])
        raw_in = [sem(f"d_raw_in{i}") for i in range(2)]
        mm, hi, lo = sem("d_mm"), sem("d_hi"), sem("d_lo")
        stored = [sem(f"d_stored{i}") for i in range(SLOTS)]

        downs = [(pr, n) for pr in range(KV_HEADS // 2) for n in range(2)]
        up_keys = [(n, hk) for n in range(2) for hk in range(KV_HEADS)]
        up_vals = [(j, n) for j in range(TB) for n in range(2)]
        PREP, DOWN, UP = 12, len(downs), len(up_keys) + len(up_vals)
        USES = DOWN + UP
        RAWS = 6
        assert USES % len(bank) == 0

        def per_slot(i):
            return len(range(i, UP, SLOTS))

        block = ctx.enter_context(nc.Block())

        def raw_src(i):
            if i < 2:
                return a[("L1_attn_Wk_down", "L1_attn_Wv_down")[i]].rearrange("(r p) c -> p r c", p=P)
            w = a[("L1_attn_Wk_up", "L1_attn_Wv_up")[i // 2 - 1]]
            return w[(i % 2) * 512:(i % 2) * 512 + 512, :].rearrange("(r p) c -> p r c", p=P)

        @block.sync
        def _(sp):
            for i in range(RAWS):
                if i >= 2:
                    sp.wait_ge(mm, 2 * (i - 1))
                src = raw_src(i)
                sp.dma_start(raw[:, i % 2, :].rearrange("p (r c) -> p r c", r=src.shape[1]), src).then_inc(raw_in[i % 2], 16)
            with sp.Fori(0, B) as b:
                for w in range(UP):
                    sp.wait_ge(lo, b * USES + (PREP + DOWN + w + 1))
                    for k, part in enumerate((st_h, st_l)):
                        src = f32(part[:, w % SLOTS, :])
                        if w < len(up_keys):
                            n, hk = up_keys[w]
                            dst = m.k_s[bass.ds(b * KV_HEADS + hk, 1), :, k, n * 512:n * 512 + 512].rearrange("g p s -> p (g s)")
                        else:
                            j, n = up_vals[w - len(up_keys)]
                            dst = m.v_s[bass.ds(b * KV_HEADS + 4 * n, 4), :, k, j, :].rearrange("g p d -> p g d")
                            src = src.rearrange("p (g d) -> p g d", g=4)
                        sp.dma_start(dst, src).then_inc(stored[w % SLOTS], 16)
            for i in range(SLOTS):
                sp.wait_ge(stored[i], 32 + B * 32 * per_slot(i))

        @block.gpsimd
        def _(pool):
            for i in range(SLOTS):
                pool.memset(f32(st_h[:, i, 0:1]), 0.0).then_inc(stored[i], 32)

        def slices(w):
            return w % SLOTS, w // SLOTS

        def turned_parts(i, bk):
            if i < 4:
                kv, t = i // 2, i % 2
                hs = slice(4 * t, 4 * t + 4)
                return (dn_h[:, :, hs, kv, :], dn_l[:, :, hs, kv, :], bk.rearrange("p (c g e) -> p c g e", c=CH, g=4))
            kv, r, c = (i - 4) // 4, (i - 4) // 2 % 2, i % 2
            cols = slice(r * 512, r * 512 + 512)
            return up_h[:, kv, c, cols], up_l[:, kv, c, cols], bk

        def latent_parts(use, bk):
            pr, n = downs[use]
            for half in range(2):
                for odd in range(2):
                    rows = slice(odd * 64, odd * 64 + 64)
                    cols = slice((2 * pr + half) * P + n * 64, (2 * pr + half) * P + n * 64 + 64)
                    src = bk[half * 64:half * 64 + 64, :].rearrange("p (t r q) -> p r q t", r=4, q=2)[:, :, odd, :]
                    yield cmp_h[rows, :, cols], cmp_l[rows, :, cols], src

        @block.scalar
        def _(act):
            for i in range(PREP):
                act.wait_ge(mm, i + 1)
                high, _, src = turned_parts(i, bank[i % 8])
                act.activation(high, src, ACT.Copy).then_inc(hi, 1)
            with act.Fori(0, B) as b:
                for use in range(USES):
                    bk = bank[(PREP + use) % 8]
                    act.wait_ge(mm, b * USES + (PREP + use + 1))
                    if use < DOWN:
                        for high, _, src in latent_parts(use, bk):
                            last = act.activation(high, src, ACT.Copy)
                        last.then_inc(hi, 1)
                    else:
                        slot, before = slices(use - DOWN)
                        act.wait_ge(stored[slot], b * (32 * per_slot(slot)) + 32 * (before + 1))
                        act.activation(st_h[:, slot, :], bk, ACT.Copy).then_inc(hi, 1)

        @block.vector
        def _(dve):
            for i in range(PREP):
                dve.wait_ge(hi, i + 1)
                high, low, src = turned_parts(i, bank[i % 8])
                dve.tensor_tensor(low, src, f32(high), ALU.subtract).then_inc(lo, 1)
            with dve.Fori(0, B) as b:
                for use in range(USES):
                    bk = bank[(PREP + use) % 8]
                    dve.wait_ge(hi, b * USES + (PREP + use + 1))
                    if use < DOWN:
                        for high, low, src in latent_parts(use, bk):
                            last = dve.tensor_tensor(low, src, f32(high), ALU.subtract)
                        last.then_inc(lo, 1)
                    else:
                        slot, _ = slices(use - DOWN)
                        dve.tensor_tensor(st_l[:, slot, :], bk, f32(st_h[:, slot, :]), ALU.subtract).then_inc(lo, 1)

        @block.tensor
        def _(pe):
            for i in range(PREP):
                if i % 2 == 0:
                    pe.wait_ge(raw_in[i // 2 % 2], 16 * (i // 4 + 1))
                if i >= 8:
                    pe.wait_ge(lo, i - 7)
                block_ = raw[:, i // 2 % 2, :]
                for k in range(4):
                    if i < 4:
                        src = block_[:, (i % 2) * HID + k * P:(i % 2) * HID + k * P + P]
                    else:
                        src = block_[:, k * LATW + (i % 2) * P:k * LATW + (i % 2) * P + P]
                    last = pe.transpose(bank[i % 8][:, k * P:(k + 1) * P], src, m.ident[:])
                last.then_inc(mm, 1)
            with pe.Fori(0, B) as b:
                for use in range(USES):
                    bk = bank[(PREP + use) % 8]
                    pe.wait_ge(lo, b * USES + (PREP + use - 7))
                    if use < DOWN:
                        pr, n = downs[use]
                        if use == 0:
                            pe.wait_ge(lo, PREP)
                        w = lambda x, c: x[:, c, 2 * pr:2 * pr + 2, :, :].rearrange("p g k e -> p (g k e)")
                        x = lambda x, c: x[:, c, bass.ds(b * S + n * 512, 512)]
                        terms = [(w(dn_h, c), w(dn_l, c), x(m.xT_h, c), x(m.xT_l, c)) for c in range(CH)]
                    elif use < DOWN + len(up_keys):
                        n, hk = up_keys[use - DOWN]
                        if hk == 0:
                            pe.wait_ge(lo, b * USES + (PREP + DOWN // 2 * (n + 1)))
                        ks, ts = slice(hk * D, hk * D + D), slice(n * 512, n * 512 + 512)
                        terms = [(up_h[:, 0, c, ks], up_l[:, 0, c, ks], cmp_h[:, c, ts], cmp_l[:, c, ts]) for c in range(LC)]
                    else:
                        j, n = up_vals[use - DOWN - len(up_keys)]
                        ts, vs = slice(j * P, j * P + P), slice(n * 512, n * 512 + 512)
                        terms = [(cmp_h[:, LC + c, ts], cmp_l[:, LC + c, ts], up_h[:, 1, c, vs], up_l[:, 1, c, vs])
                                 for c in range(LC)]
                    mm3(pe, bk, terms).then_inc(mm, 1)


def layer1_attention(nc, a, m, bank, bank2, out):
    with ExitStack() as ctx:
        def sb(name, shape, dt=F32):
            return ctx.enter_context(nc.sbuf_tensor(name, shape, dt))

        def sem(name):
            return ctx.enter_context(nc.semaphore(name))

        HALF = S // 2
        xT = sb("x_batch", [P, 2, CH, S], F32R)
        wq = sb("wq", [P, 2, CH, REP * D], F32R)
        wo = sb("wo", [P, 2, REP, HID], F32R)
        keys = sb("keys", [P, 2, S], F32R)
        vals = sb("vals", [P, 2, TB, D], F32R)
        q = sb("q", [P, 2, REP, S], F32R)
        probs = sb("probs", [P, 2, REP, S])
        PT_SLOTS = 3
        pT = sb("pT", [P, PT_SLOTS, 2, REP * P], F32R)
        oT = sb("oT", [P, 2, 2, REP * P], F32R)
        free = sb("free", [P, 4])
        nmax, rsum, rinv = (sb(n, [P, TB, REP]) for n in ("nmax", "rsum", "rinv"))

        x_in = [sem("e_x_in_low"), sem("e_x_in_high")]
        wq_in, wo_in, k_in = sem("e_wq_in"), sem("e_wo_in"), sem("e_k_in")
        v_in = [sem("e_v_in_low"), sem("e_v_in_high")]
        q_mm, q_hi, q_lo = sem("e_q_mm"), sem("e_q_hi"), sem("e_q_lo")
        s_mm, s_max, p_exp, p_inv, p_ok, p_last = (sem("e_" + n) for n in ("s_mm", "s_max", "p_exp", "p_inv", "p_ok", "p_last"))
        t_mm, t_hi, t_lo, pv_mm = (sem("e_" + n) for n in ("t_mm", "t_hi", "t_lo", "pv_mm"))
        o_hi, o_lo, w_mm, x_add = (sem("e_" + n) for n in ("o_hi", "o_lo", "w_mm", "x_add"))
        stored = sem("e_stored")

        ITERS = B * KV_HEADS
        QS = 2 * REP
        SC = TB * REP
        TILES = TB * (TB + 1) // 2
        T0, PV0, O0, X0 = 2, PT_SLOTS, 1, 1

        def first_tile(u):
            return sum(TB - k for k in range(u))

        T_BANK, O_BANK, W_BANK = 4, 6, 7

        def w_bank(u):
            return bank[W_BANK if u < TB - 2 else T_BANK + u % 2]

        def q_bank(k):
            return bank[T_BANK + k if k < REP else W_BANK]

        def q_place(k):
            return k % REP, slice(0, HALF) if k < REP else slice(HALF, S)

        def columns(u):
            n = (TB - u) * P
            off = P if n == 512 + P else 0
            cuts = [0] + ([512 - off] if n + off > 512 else []) + [n]
            return off, n, list(zip(cuts, cuts[1:]))

        LAG = 2
        QUERY_UNIT = 5

        def steps(last):
            order, due = [], []

            def emit(*step):
                if step[0] == "turn" and step[2] == 0:
                    ours = [d for d in due if d[1][0] in ("probs", "norm") and d[1][1] == step[1]]
                    for d in ours:
                        due.remove(d)
                        order.append(d[1])
                order.append(step)
                for d in due:
                    d[0] -= 1
                while due and due[0][0] <= 0:
                    order.append(due.pop(0)[1])

            def later(n, *step):
                due.append([n, step])
                due.sort(key=lambda d: d[0])

            def flush():
                while due:
                    order.append(due.pop(0)[1])

            def scores(u, h, behind=2, then=2, maximum=0):
                emit("scores", u, h)
                if maximum:
                    later(maximum, "max", u, h)
                else:
                    order.append(("max", u, h))
                later(maximum + behind, "probs", u, h)
                later(maximum + behind + then, "norm", u, h)

            def project(u):
                emit("project", u)
                later(3, "add", u)

            def run(ops):
                for op in ops:
                    emit(*op)

            def query(k, then=1):
                emit("query", k)
                later(then, "qparts", k)

            for h in range(2):
                scores(0, h, 1)
            query(0)
            query(1)
            scores(0, 2, 1)
            scores(0, 3, 1, 1)
            query(2, 2)
            for u in range(1, TB):
                n = TB - u + 1
                turns = [("turn", u - 1, k) for k in range(n)]
                rest = []
                for k in range(n):
                    rest += turns[k + LAG:k + LAG + 1] + [("weigh", u - 1, k)]
                first, second = len(rest) // 3, len(rest) * 2 // 3
                scores(u, 0, 1)
                scores(u, 1)
                run(turns[:LAG])
                if u == 1:
                    query(3)
                else:
                    project(u - 2)
                    run(rest[:first] if u < TB - 1 else [])
                if u < TB - 1:
                    scores(u, 2)
                    run(rest[first if u > 1 else 0:second])
                    scores(u, 3)
                    run(rest[second:])
                else:
                    scores(u, 2)
                    scores(u, 3)
                    run(rest)
                if u == TB - 1:
                    flush()
                emit("heads", u - 1)
                if u >= 4 and not last and u < TB - 1:
                    query(REP + u - 4)
            if not last:
                emit("query", 7)
            emit("turn", u, 0)
            project(u - 1)
            emit("weigh", u, 0)
            emit("heads", u)
            if not last:
                emit("query", 7.5)
                emit("qparts", 7)
            project(u)
            flush()
            return order

        block = ctx.enter_context(nc.Block())

        @block.sync
        def _(sp):
            def load(dst, src):
                return sp.dma_start(f32(dst), src)

            def one(t, i):
                return t[bass.ds(i, 1)].rearrange("g p k x y -> p (g k) x y" if len(t.shape) == 5 else "g p k x -> p (g k) x")

            def loads(it, bg, g):
                sp.wait_ge(q_mm, it * QS + QS)
                load(wq[:], one(m.wq_s, g)).then_inc(wq_in, 16)
                sp.wait_ge(pv_mm, it * TILES + (PV0 + first_tile(4)))
                load(vals[:, :, 4:8, :], one(m.v_s, bg)[:, :, 4:8, :]).then_inc(v_in[1], 16)
                sp.wait_ge(s_mm, it * SC + SC)
                for k in (1, 0):
                    load(keys[:, k, :], m.k_s[bass.ds(bg, 1), :, k, :].rearrange("g p s -> p (g s)")).then_inc(k_in, 16)
                sp.wait_ge(pv_mm, it * TILES + (PV0 + TILES))
                load(vals[:, :, 0:4, :], one(m.v_s, bg)[:, :, 0:4, :]).then_inc(v_in[0], 16)
                sp.wait_ge(w_mm, it * TB + TB)
                load(wo[:], one(m.wo_s, g)).then_inc(wo_in, 16)

            load(wq[:], m.wq_s[0]).then_inc(wq_in, 16)
            for half in (1, 0):
                cols = slice(half * HALF, half * HALF + HALF)
                load(xT[:, :, :, cols].rearrange("p k c s -> p (k c) s"),
                     m.xT_s[0, :, :, :, cols].rearrange("p k c s -> p (k c) s")).then_inc(x_in[half], 16)
                if half:
                    load(keys[:], m.k_s[0]).then_inc(k_in, 32)
            for half in (1, 0):
                load(vals[:, :, 4 * half:4 * half + 4, :], m.v_s[0, :, :, 4 * half:4 * half + 4, :]).then_inc(v_in[half], 16)
            load(wo[:], m.wo_s[0]).then_inc(wo_in, 16)
            G = KV_HEADS
            with sp.Fori(0, G - 1) as it:
                loads(it, it + 1, it + 1)
            sp.wait_ge(q_mm, QS * (G - 1) + QS)
            load(xT[:].rearrange("p k c s -> p (k c s)"), m.xT_s[1].rearrange("p k c s -> p (k c s)")).then_inc(x_in[0], 16)
            sp.wait_ge(x_in[0], 32)
            loads(G - 1, G, 0)
            sp.wait_ge(x_add, X0 + TB * G)
            sp.dma_start(out[0].rearrange("(t p) c -> p t c", p=P), m.acc[:, 0:TB, :]).then_inc(stored, 16)
            with sp.Fori(0, G - 1) as g:
                loads(g + G, g + (G + 1), g + 1)
            for u in range(TB):
                i = TB - 1 - u
                sp.wait_ge(x_add, X0 + TB * (ITERS - 1) + u + 1)
                sp.dma_start(out[1, i * P:i * P + P, :], m.acc[:, TB + i, :]).then_inc(stored, 16)
            sp.wait_ge(stored, 16 * (1 + TB))

        @block.gpsimd
        def _(pool):
            pool.memset(free[:, 0:1], 0.0).then_inc(t_lo, T0)
            pool.memset(free[:, 1:2], 0.0).then_inc(pv_mm, PV0)
            pool.memset(free[:, 2:3], 0.0).then_inc(o_lo, O0)
            pool.memset(free[:, 3:4], 0.0).then_inc(x_add, X0)

            def body(it, last):
                for kind, *arg in steps(last):
                    if kind == "norm" and arg[1] < REP - 1:
                        u, h = arg
                        p = probs[:, u % 2, h, 0:(TB - u) * P]
                        pool.wait_ge(p_inv, it * SC + (REP * u + h + 1))
                        pool.tensor_tensor(p, p, rinv[:, u, h:h + 1].to_broadcast([P, (TB - u) * P]), ALU.mult).then_inc(p_ok, 1)

            with pool.Fori(0, ITERS - 1) as it:
                body(it, False)
            body(ITERS - 1, True)

        @block.vector
        def _(dve):
            def query_low(k, n):
                h, cols = q_place(k)
                dve.wait_ge(q_hi, n)
                dve.scalar_tensor_tensor(out=q[:, 1, h, cols], in0=q_bank(k), scalar=SCALE, in1=f32(q[:, 0, h, cols]),
                                         op0=ALU.mult, op1=ALU.subtract).then_inc(q_lo, 1)

            def body(it, b, last):
                for kind, *arg in steps(last):
                    u = arg[0]
                    if kind == "max":
                        h = arg[1]
                        off, n, _ = columns(u)
                        dve.wait_ge(s_mm, it * SC + (REP * u + h + 1))
                        dve.tensor_reduce(nmax[:, u, h:h + 1], bank2[2 * (h % 2)][:, off:off + n], AX.X, ALU.max,
                                          negate=True).then_inc(s_max, 1)
                    elif kind == "norm":
                        h = arg[1]
                        dve.wait_ge(p_exp, it * SC + (REP * u + h + 1))
                        dve.reciprocal(rinv[:, u, h:h + 1], rsum[:, u, h:h + 1]).then_inc(p_inv, 1)
                        if h == REP - 1:
                            p = probs[:, u % 2, h, 0:(TB - u) * P]
                            dve.wait_ge(p_inv, it * SC + (REP * u + h + 1))
                            dve.tensor_scalar(p, p, rinv[:, u, h:h + 1], None, ALU.mult).then_inc(p_last, 1)
                    elif kind == "turn":
                        n = first_tile(u) + arg[1]
                        dve.wait_ge(t_hi, it * TILES + (n + 1))
                        dve.tensor_tensor(pT[:, n % PT_SLOTS, 1, :], bank[T_BANK + n % 2], f32(pT[:, n % PT_SLOTS, 0, :]),
                                          ALU.subtract).then_inc(t_lo, 1)
                    elif kind == "heads":
                        dve.wait_ge(o_hi, it * TB + (u + 1))
                        dve.tensor_tensor(oT[:, u % 2, 1, :], bank[O_BANK], f32(oT[:, u % 2, 0, :]), ALU.subtract).then_inc(o_lo, 1)
                    elif kind == "add":
                        x = m.acc[:].rearrange("p (b t) c -> p b t c", b=B)[:, bass.ds(b, 1), TB - 1 - u, :].rearrange("p b c -> p (b c)")
                        dve.wait_ge(w_mm, it * TB + (u + 1))
                        dve.tensor_tensor(x, x, w_bank(u), ALU.add).then_inc(x_add, 1)
                    elif kind == "qparts":
                        query_low(u, it * QS + (REP + u + 1))

            for k in range(REP):
                query_low(REP + k, k + 1)
            with dve.Fori(0, ITERS - 1) as it:
                b = nc.s_assert_within(it >> 3, 0, B - 1, skip_runtime_bounds_check_because="it is below 16")
                body(it, b, False)
            body(ITERS - 1, B - 1, True)

        @block.scalar
        def _(act):
            def query_high(k, n):
                h, cols = q_place(k)
                act.wait_ge(q_mm, n)
                act.activation(q[:, 0, h, cols], q_bank(k), ACT.Copy, scale=SCALE).then_inc(q_hi, 1)

            def body(it, last):
                for kind, *arg in steps(last):
                    u = arg[0]
                    if kind == "probs":
                        h = arg[1]
                        off, n, _ = columns(u)
                        act.wait_ge(s_max, it * SC + (REP * u + h + 1))
                        act.activation(probs[:, u % 2, h, 0:n], bank2[2 * (h % 2)][:, off:off + n], ACT.Exp,
                                       bias=nmax[:, u, h:h + 1], accum_out=rsum[:, u, h:h + 1]).then_inc(p_exp, 1)
                    elif kind == "turn":
                        n = first_tile(u) + arg[1]
                        act.wait_ge(pv_mm, it * TILES + (n + 1))
                        act.wait_ge(t_mm, it * TILES + (n + 1))
                        act.activation(pT[:, n % PT_SLOTS, 0, :], bank[T_BANK + n % 2], ACT.Copy).then_inc(t_hi, 1)
                    elif kind == "heads":
                        act.wait_ge(pv_mm, it * TILES + (PV0 + first_tile(u + 1)))
                        act.activation(oT[:, u % 2, 0, :], bank[O_BANK], ACT.Copy).then_inc(o_hi, 1)
                    elif kind == "qparts":
                        query_high(u, it * QS + (REP + u + 1))

            for k in range(REP):
                query_high(REP + k, k + 1)
            with act.Fori(0, ITERS - 1) as it:
                body(it, False)
            body(ITERS - 1, True)

        @block.tensor
        def _(pe):
            def queries(k, chunks):
                h, cols = q_place(k)
                hs = slice(h * D, h * D + D)
                return mm3(pe, q_bank(k), [(wq[:, 0, c, hs], wq[:, 1, c, hs], xT[:, 0, c, cols], xT[:, 1, c, cols]) for c in chunks],
                           start=0 in chunks, stop=CH - 1 in chunks)

            def body(it, last):
                for kind, *arg in steps(last):
                    u = arg[0]
                    if kind == "scores":
                        h = arg[1]
                        i = TB - 1 - u
                        e = REP * u + h
                        if e == 0:
                            pe.wait_ge(k_in, it * 32 + 32)
                            pe.wait_ge(q_lo, it * QS + REP)
                        elif e >= 2:
                            pe.wait_ge(p_exp, it * SC + (e - 1))
                        if e == REP * 4:
                            pe.wait_ge(q_lo, it * QS + 2 * REP)
                        off, n, cuts = columns(u)
                        slot = bank2[2 * (h % 2)]
                        qs = slice(i * P, i * P + P)
                        for lo, hi in cuts:
                            mm3(pe, slot[:, off + lo:off + hi], [(q[:, 0, h, qs], q[:, 1, h, qs], keys[:, 0, lo:hi], keys[:, 1, lo:hi])],
                                stop=hi < n)
                        pe.matmul(slot[:, off + n - P:off + n], m.identb[:], m.maskb[:], start=False, stop=True).then_inc(s_mm, 1)
                    elif kind == "turn":
                        k = arg[1]
                        n, j = first_tile(u) + k, TB - 1 - u - k
                        if k == 0:
                            pe.wait_ge(p_ok, it * ((REP - 1) * TB) + (REP - 1) * (u + 1))
                            pe.wait_ge(p_last, it * TB + (u + 1))
                            if u == 0:
                                pe.wait_ge(q_lo, it * QS + (REP + 2))
                        pe.wait_ge(t_lo, it * TILES + (T0 + n - 1))
                        for h in range(REP):
                            ins = pe.transpose(bank[T_BANK + n % 2][:, h * P:(h + 1) * P], probs[:, u % 2, h, j * P:(j + 1) * P], m.ident[:])
                        ins.then_inc(t_mm, 1)
                    elif kind == "weigh":
                        k = arg[1]
                        n, j = first_tile(u) + k, TB - 1 - u - k
                        if k == 0:
                            pe.wait_ge(o_lo, it * TB + (O0 + u))
                            if u == 0:
                                pe.wait_ge(q_lo, it * QS + (REP + 3))
                                for i in range(2):
                                    pe.wait_ge(v_in[i], it * 16 + 16)
                        pe.wait_ge(t_lo, it * TILES + (T0 + n + 1))
                        mm3(pe, bank[O_BANK], [(vals[:, 0, j, :], vals[:, 1, j, :], pT[:, n % PT_SLOTS, 0, :], pT[:, n % PT_SLOTS, 1, :])],
                            start=k == 0, stop=j == 0).then_inc(pv_mm, 1)
                    elif kind == "project":
                        if u == 0:
                            pe.wait_ge(wo_in, it * 16 + 16)
                        pe.wait_ge(o_lo, it * TB + (O0 + u + 1))
                        pe.wait_ge(x_add, it * TB + (X0 + u))
                        if u == 0 or 3 <= u < TB - 2 and not last:
                            pe.wait_ge(q_lo, it * QS + (2 * REP + max(u - 2, 0)))
                        mm3(pe, w_bank(u), [(oT[:, u % 2, 0, h * P:(h + 1) * P], oT[:, u % 2, 1, h * P:(h + 1) * P],
                                             wo[:, 0, h, :], wo[:, 1, h, :]) for h in range(REP)]).then_inc(w_mm, 1)
                    elif kind == "query":
                        if u == 0:
                            pe.wait_ge(x_add, it * TB + X0)
                        elif u == 2:
                            pe.wait_ge(o_lo, it * TB + O0)
                        elif u >= REP:
                            if u == REP:
                                pe.wait_ge(wq_in, it * 16 + 32)
                            pe.wait_ge(x_add, it * TB + (X0 + int(u) - 1))
                        if u < QS - 1:
                            queries(u, range(CH)).then_inc(q_mm, 1)
                        elif u == QS - 1:
                            queries(u, range(1))
                        else:
                            queries(int(u), range(1, CH)).then_inc(q_mm, 1)

            pe.wait_ge(wq_in, 16)
            pe.wait_ge(x_in[1], 16)
            for k in range(REP):
                if k:
                    pe.wait_ge(q_lo, k)
                queries(REP + k, range(CH)).then_inc(q_mm, 1)
            pe.wait_ge(x_in[0], 16)
            with pe.Fori(0, ITERS - 1) as it:
                body(it, False)
            body(ITERS - 1, True)
def program(nc, a, out):
    with ExitStack() as ctx:
        def sb(name, shape, dt=F32):
            return ctx.enter_context(nc.sbuf_tensor(name, shape, dt))

        def pair(stack, name, shape):
            return [stack.enter_context(nc.sbuf_tensor(name + s, shape, F32R)) for s in ("_h", "_l")]

        psum = ctx.enter_context(nc.psum_tensor("psum", [P, 8 * 512], F32))
        bank = [psum[:, 512 * i:512 * i + 512] for i in range(8)]
        bank2 = [psum[:, 512 * i:512 * i + 1024] for i in range(7)]
        m = Shared()
        m.acc = sb("acc", [P, NT, HID])
        m.ident = sb("ident", [P, P])
        m.identb = sb("identb", [P, P], BF16)
        m.maskb = sb("maskb", [P, P], BF16)
        m.ones = sb("ones", [P, P])
        m.wq_s = nc.dram_tensor("wq_parts", (KV_HEADS, P, 2, CH, REP * D), F32, kind="Internal").ap()
        m.wo_s = nc.dram_tensor("wo_parts", (KV_HEADS, P, 2, REP, HID), F32, kind="Internal").ap()
        m.k_s = nc.dram_tensor("k_parts", (B * KV_HEADS, P, 2, S), F32, kind="Internal").ap()
        m.v_s = nc.dram_tensor("v_parts", (B * KV_HEADS, P, 2, TB, D), F32, kind="Internal").ap()
        m.xT_s = nc.dram_tensor("x_parts", (B, P, 2, CH, S), F32, kind="Internal").ap()
        with ExitStack() as layer0:
            m.xn0 = layer0.enter_context(nc.sbuf_tensor("xn0", [P, NT, HID], F32))
            m.logits = layer0.enter_context(nc.sbuf_tensor("logits", [P, NT, NLOG], F32))
            m.q0_h, m.q0_l = pair(layer0, "q0", [P, N])
            m.k0_h, m.k0_l = pair(layer0, "k0", [P, N])
            m.v0_h, m.v0_l = pair(layer0, "v0", [P, NT, D])
            layer0_project(nc, a, m, bank)
            layer0_mix(nc, a, m, bank, bank2)
        with ExitStack() as layer1:
            m.xT_h, m.xT_l = pair(layer1, "xT", [P, CH, N])
            layer1_ffn(nc, a, m, bank)
            layer1_keys(nc, a, m, bank)
        layer1_attention(nc, a, m, bank, bank2, out)


_INS = ['L0_attn_x', 'L0_attn_Wqkv', 'L0_attn_bqkv', 'L0_attn_Wo', 'L0_attn_bo', 'L0_ffn_W_res', 'L0_ffn_W_pre',
        'L0_ffn_W_post', 'L0_ffn_H_res_base', 'L0_ffn_H_pre_base', 'L0_ffn_H_post_base', 'L0_ffn_gate',
        'L0_ffn_W_branch', 'L1_attn_Wq', 'L1_attn_Wk_down', 'L1_attn_Wv_down', 'L1_attn_Wk_up', 'L1_attn_Wv_up',
        'L1_attn_Wo', 'L1_ffn_weight', 'L1_ffn_lora_A', 'L1_ffn_lora_B', 'L1_ffn_gw1', 'L1_ffn_gb1',
        'L1_ffn_ln_gamma', 'L1_ffn_ln_beta', 'L1_ffn_gw2', 'L1_ffn_gb2']


def kernel(**inputs):
    import numpy as np
    import concourse.bacc as bacc
    from concourse.bass_utils import run_bass_kernel_spmd

    nc = bacc.Bacc("TRN2", target_bir_lowering=False, num_devices=1)
    arrays, aps = {}, {}
    for name in _INS:
        x = np.ascontiguousarray(inputs[name])
        arrays["in_" + name] = x
        aps[name] = nc.dram_tensor("in_" + name, x.shape, mybir.dt.from_np(x.dtype), kind="ExternalInput").ap()
    out = nc.dram_tensor("out_x", (B, S, HID), F32, kind="ExternalOutput").ap()
    program(nc, aps, out)
    r = run_bass_kernel_spmd(nc, [arrays], core_ids=[0])
    return r.results[0]["out_x"]
```

```python
from contextlib import ExitStack

import concourse.bass as bass
from concourse import mybir

F32 = mybir.dt.float32
F32R = mybir.dt.float32r
BF16 = mybir.dt.bfloat16
ALU = mybir.AluOpType
ACT = mybir.ActivationFunctionType
AX = mybir.AxisListType

P = 128
B, S, HID = 2, 1024, 512
N = B * S
NT = N // P
TB = S // P
CH = HID // P
D = 128
LN_EPS = 1e-5
RMS_EPS = 1.1920929e-07
NS = 4
NZ = NS * NS
NLOG = NZ + 2 * NS
TAU = 0.1
SINKHORN_ITERS = 50
SINKHORN_CHUNK = 25
HEADS, KV_HEADS = 32, 8
REP = HEADS // KV_HEADS
LAT = D // 4
LATW = KV_HEADS * LAT
LC = LATW // P
KVW = KV_HEADS * D
EXP, TOPK, RANK = 8, 2, 16
GH = 4 * EXP
ALPHA = 1.0 / RANK
CAPACITY = int(3.0 * N / EXP)
SCALE = float(D) ** -0.5
MASKED = -1e30


class Shared:
    pass


def mm3(pe, out, terms, start=True, stop=True):
    n = len(terms)
    for i, (wh, wl, xh, xl) in enumerate(terms):
        pe.matmul(out, wh, xh, start=start and i == 0, stop=False)
        pe.matmul(out, wh, xl, start=False, stop=False)
        last = pe.matmul(out, wl, xh, start=False, stop=stop and i == n - 1)
    return last


def f32(ap):
    return ap.bitcast(F32)


def split_weights(pool, m, w, k, n, ok):
    pool.tensor_tensor(w[:, 0, k, :], f32(w[:, 1, k, :]), m.zero[:].to_broadcast([P, w.shape[3]]), ALU.add).then_inc(m.w_hi, 1)
    pool.wait_ge(m.w_hi, n)
    pool.tensor_tensor(w[:, 1, k, :], f32(w[:, 1, k, :]), f32(w[:, 0, k, :]), ALU.subtract).then_inc(ok, 1)


def layer0_project(nc, a, m, bank):
    with ExitStack() as ctx:
        def sb(name, shape, dt=F32):
            return ctx.enter_context(nc.sbuf_tensor(name, shape, dt))

        def pair(name, shape):
            return sb(name + "_h", shape, F32R), sb(name + "_l", shape, F32R)

        def sem(name):
            return ctx.enter_context(nc.semaphore(name))

        xT0_h, xT0_l = pair("xT0", [P, CH, N])
        wqkv = m.xn0[:, NT - 3:NT, :].rearrange("p t c -> p (t c)").rearrange("p (c f) -> p c f", c=CH)
        wqkv2_h, wqkv2_l = pair("wqkv2", [P, CH, 3 * D])
        wlog = sb("wlog", [NLOG, HID])
        wlogT_h, wlogT_l = pair("wlogT", [P, CH, P])
        bqkv = sb("bqkv", [P, 3])
        bo = sb("bo", [P, HID])
        zbase = sb("zbase", [P, NLOG])
        st = sb("st0", [P, NT, 6])
        mv = sb("mv0", [P, NT, 2])
        rstd = sb("rstd0", [P, NT])
        ssq = sb("ssq0", [P, NT])
        rms = sb("rms0", [P, NT])
        tmpv = sb("tmpv0", [P, 2, NT])
        mhalf = sb("mhalf0", [P, NT])
        junk = sb("junk0", [P, HID], BF16)
        vT = sb("vT0", [P, 512])
        lgT = sb("lgT0", [NLOG, 512])
        xn, x1 = m.xn0, m.acc

        x_in = [sem(f"a_x_in{n}") for n in range(4)]
        w_in, const = sem("a_w_in"), sem("a_const")
        st_done, mv_done, var_eps, rstd_ok, xn_ok = sem("a_st"), sem("a_mv"), sem("a_var"), sem("a_rstd"), sem("a_xn")
        ssq_ok, rms_in, rms_ok = sem("a_ssq"), sem("a_rmsin"), sem("a_rms")
        wl_mm, wl_hi, wl_lo, wq_hi, wq_lo = sem("a_wlmm"), sem("a_wlhi"), sem("a_wllo"), sem("a_wqhi"), sem("a_wqlo")
        xT_mm, xT_hi, xT_lo = sem("a_xTmm"), sem("a_xThi"), sem("a_xTlo")
        job_mm, qk_ok = sem("a_jobmm"), sem("a_qk")
        vT_ok, lgT_ok = sem("a_vT"), sem("a_lgT")
        v_mm, v_ok, lg_mm, lg_ok = sem("a_vmm"), sem("a_v"), sem("a_lgmm"), sem("a_lg")
        TQ = 4
        W_LOADS = 11

        block = ctx.enter_context(nc.Block())

        @block.sync
        def _(sp):
            for n in range(4):
                sp.dma_start(x1[:, TQ * n:TQ * n + TQ, :],
                             a["L0_attn_x"].rearrange("b s c -> (b s) c")[512 * n:512 * n + 512, :]
                             .rearrange("(t p) c -> p t c", p=P)).then_inc(x_in[n], 16)

        @block.gpsimd
        def _(pool):
            pool.memset(m.ident[:], 0.0).then_inc(const, 1)
            pool.memset(m.maskb[:], 0.0).then_inc(const, 1)
            pool.memset(m.ones[:], 1.0).then_inc(const, 1)
            pool.memset(m.zero[:], 0.0).then_inc(const, 1)
            pool.memset(mhalf[:], -0.5).then_inc(const, 1)
            pool.memset(f32(wlogT_h[:]), 0.0).then_inc(const, 1)
            pool.memset(f32(wlogT_l[:]), 0.0).then_inc(const, 1)
            pool.wait_ge(const, 7)
            pool.affine_select(out=m.ident[:], in_=m.ident[:], compare_op=ALU.not_equal, fill=1.0,
                               base=0, pattern=[[-1, P]], channel_multiplier=1).then_inc(const, 1)
            pool.affine_select(out=m.maskb[:], in_=m.maskb[:], compare_op=ALU.is_ge, fill=MASKED,
                               base=0, pattern=[[-1, P]], channel_multiplier=1).then_inc(const, 1)
            pool.wait_ge(const, 9)
            pool.tensor_copy(m.identb[:], m.ident[:]).then_inc(const, 1)
            pool.wait_ge(wq_hi, 1)
            pool.tensor_tensor(wqkv2_l[:], wqkv, f32(wqkv2_h[:]), ALU.subtract).then_inc(wq_lo, 1)

            def rms_of(n):
                cols = slice(TQ * n, TQ * n + TQ)
                pool.wait_ge(ssq_ok, TQ * (n + 1))
                pool.tensor_scalar(tmpv[:, 1, cols], ssq[:, cols], 1.0 / HID, RMS_EPS, ALU.mult,
                                   ALU.add).then_inc(rms_in, 1)
                pool.wait_ge(rms_in, n + 1)
                pool.tensor_tensor(rms[:, cols], tmpv[:, 1, cols], mhalf[:, cols], ALU.pow).then_inc(rms_ok, 1)

            for n in range(4):
                cols = slice(TQ * n, TQ * n + TQ)
                pool.wait_ge(mv_done, TQ * (n + 1))
                pool.tensor_scalar(tmpv[:, 0, cols], mv[:, cols, 1], 1.0, LN_EPS, ALU.mult,
                                   ALU.add).then_inc(var_eps, 1)
                pool.wait_ge(var_eps, n + 1)
                pool.tensor_tensor(rstd[:, cols], tmpv[:, 0, cols], mhalf[:, cols], ALU.pow).then_inc(rstd_ok, 1)
                if n:
                    rms_of(n - 1)
            rms_of(3)
            pool.wait_ge(w_in, 16 * W_LOADS)
            for t in range(NT):
                pool.wait_ge(xn_ok, t + 1)
                pool.tensor_tensor(x1[:, t, :], x1[:, t, :], bo[:], ALU.add)

        @block.vector
        def _(dve):
            def stats(n):
                dve.wait_ge(x_in[n], 16)
                for t in range(TQ * n, TQ * n + TQ):
                    dve.bn_stats(st[:, t, :], x1[:, t, :]).then_inc(st_done, 1)
                for t in range(TQ * n, TQ * n + TQ):
                    dve.wait_ge(st_done, t + 1)
                    dve.bn_aggr(mv[:, t, :], st[:, t, :]).then_inc(mv_done, 1)

            def norm(n):
                dve.wait_ge(rstd_ok, n + 1)
                if n == 3:
                    dve.wait_ge(wq_lo, 1)
                for t in range(TQ * n, TQ * n + TQ):
                    if t == TQ * n:
                        dve.wait_ge(mv_done, TQ * n + TQ)
                    dve.tensor_scalar(xn[:, t, :], x1[:, t, :], mv[:, t, 0:1], rstd[:, t:t + 1], ALU.subtract,
                                      ALU.mult).then_inc(xn_ok, 1)

            def low_xT(n):
                for t in range(TQ * n, TQ * n + TQ):
                    dve.wait_ge(xT_hi, t + 1)
                    cols = slice(t * P, t * P + P)
                    dve.tensor_tensor(xT0_l[:, :, cols], bank[t % 2][:].rearrange("p (c t) -> p c t", c=CH),
                                      f32(xT0_h[:, :, cols]), ALU.subtract).then_inc(xT_lo, 1)

            def post(n):
                dve.wait_ge(rms_ok, n + 1)
                dve.wait_ge(lg_mm, n + 1)
                for k in range(TQ):
                    t = TQ * n + k
                    dve.scalar_tensor_tensor(out=m.logits[:, t, :], in0=bank[7][:, k * NLOG:(k + 1) * NLOG],
                                             scalar=rms[:, t:t + 1], in1=zbase[:], op0=ALU.mult,
                                             op1=ALU.add).then_inc(lg_ok, 1)

            stats(0)
            dve.wait_ge(w_in, 16 * W_LOADS)
            dve.wait_ge(wl_hi, 1)
            dve.tensor_tensor(wlogT_l[:, :, 0:NLOG], bank[7][:, 0:CH * NLOG].rearrange("p (c n) -> p c n", c=CH),
                              f32(wlogT_h[:, :, 0:NLOG]), ALU.subtract).then_inc(wl_lo, 1)
            for s in range(6):
                if s < 3:
                    stats(s + 1)
                if s < 4:
                    norm(s)
                    low_xT(s)
                if s >= 2:
                    post(s - 2)

        @block.scalar
        def _(act):
            for dst, src in ((wqkv, a["L0_attn_Wqkv"].rearrange("(c p) f -> p c f", p=P)),
                             (wlog[0:NZ, :], a["L0_ffn_W_res"]), (wlog[NZ:NZ + NS, :], a["L0_ffn_W_pre"]),
                             (wlog[NZ + NS:NLOG, :], a["L0_ffn_W_post"]),
                             *((bqkv[:, k:k + 1], a["L0_attn_bqkv"][k * D:k * D + D].rearrange("(d o) -> d o", o=1))
                               for k in range(3)),
                             (bo[:], a["L0_attn_bo"].partition_broadcast(P)),
                             (zbase[:, 0:NZ], a["L0_ffn_H_res_base"].rearrange("i j -> (i j)").partition_broadcast(P)),
                             (zbase[:, NZ:NZ + NS], a["L0_ffn_H_pre_base"].partition_broadcast(P)),
                             (zbase[:, NZ + NS:NLOG], a["L0_ffn_H_post_base"].partition_broadcast(P))):
                act.dma_start(dst, src).then_inc(w_in, 16)
            act.wait_ge(w_in, 16 * W_LOADS)
            act.activation(wqkv2_h[:], wqkv, ACT.Copy).then_inc(wq_hi, 1)
            act.wait_ge(const, 7)
            act.wait_ge(wl_mm, 1)
            act.activation(wlogT_h[:, :, 0:NLOG], bank[7][:, 0:CH * NLOG].rearrange("p (c n) -> p c n", c=CH),
                           ACT.Copy).then_inc(wl_hi, 1)

            def high_xT(n):
                for t in range(TQ * n, TQ * n + TQ):
                    act.wait_ge(xT_mm, t + 1)
                    act.activation(xT0_h[:, :, t * P:t * P + P], bank[t % 2][:].rearrange("p (c t) -> p c t", c=CH),
                                   ACT.Copy).then_inc(xT_hi, 1)
                for t in range(TQ * n, TQ * n + TQ):
                    act.wait_ge(xn_ok, t + 1)
                    if t:
                        act.wait_ge(ssq_ok, t)
                    act.activation(junk[:], xn[:, t, :], ACT.Square, accum_out=ssq[:, t:t + 1]).then_inc(ssq_ok, 1)

            def jobs(n):
                cols = slice(512 * n, 512 * n + 512)
                for k, h in enumerate((m.q0, m.k0)):
                    act.wait_ge(job_mm, 4 * n + k + 1)
                    act.activation(h[:, cols], bank[2 + k][:], ACT.Identity, bias=bqkv[:, k:k + 1]).then_inc(qk_ok, 1)
                act.wait_ge(job_mm, 4 * n + 3)
                if n:
                    act.wait_ge(v_mm, n)
                act.activation(vT[:], bank[4][:], ACT.Identity, bias=bqkv[:, 2:3]).then_inc(vT_ok, 1)
                act.wait_ge(job_mm, 4 * n + 4)
                if n:
                    act.wait_ge(lg_mm, n)
                act.activation(lgT[:], bank[5][0:NLOG, :], ACT.Copy).then_inc(lgT_ok, 1)

            def post(n):
                act.wait_ge(v_mm, n + 1)
                act.activation(m.v0[:, TQ * n:TQ * n + TQ, :], bank[6][:].rearrange("p (t d) -> p t d", t=TQ),
                               ACT.Copy).then_inc(v_ok, 1)

            for s in range(6):
                if s < 4:
                    high_xT(s)
                if 1 <= s <= 4:
                    jobs(s - 1)
                if s >= 2:
                    post(s - 2)

        @block.tensor
        def _(pe):
            pe.wait_ge(const, 10)
            pe.wait_ge(w_in, 16 * W_LOADS)
            for c in range(CH):
                last = pe.transpose(bank[7][:, c * NLOG:(c + 1) * NLOG], wlog[:, c * P:(c + 1) * P], m.ident[0:NLOG, 0:NLOG])
            last.then_inc(wl_mm, 1)

            def turn_x(n):
                for t in range(TQ * n, TQ * n + TQ):
                    pe.wait_ge(xn_ok, t + 1)
                    if t >= 2:
                        pe.wait_ge(xT_lo, t - 1)
                    for c in range(CH):
                        last = pe.transpose(bank[t % 2][:, c * P:(c + 1) * P], xn[:, t, c * P:(c + 1) * P], m.ident[:])
                    last.then_inc(xT_mm, 1)

            def jobs(n):
                cols = slice(512 * n, 512 * n + 512)
                pe.wait_ge(xT_lo, TQ * (n + 1))
                if n == 0:
                    pe.wait_ge(wq_lo, 1)
                    pe.wait_ge(wl_lo, 1)
                for k in range(4):
                    if n:
                        pe.wait_ge((qk_ok, qk_ok, vT_ok, lgT_ok)[k], (2 * n - 1, 2 * n, n, n)[k])
                    wh, wl = (wqkv2_h, wqkv2_l) if k < 3 else (wlogT_h, wlogT_l)
                    out = slice(k * D, k * D + D) if k < 3 else slice(0, P)
                    mm3(pe, bank[2 + k][:], [(wh[:, c, out], wl[:, c, out], xT0_h[:, c, cols], xT0_l[:, c, cols])
                                             for c in range(CH)]).then_inc(job_mm, 1)

            def post(n):
                pe.wait_ge(vT_ok, n + 1)
                if n:
                    pe.wait_ge(v_ok, n)
                for k in range(TQ):
                    last = pe.transpose(bank[6][:, k * D:k * D + D], vT[:, k * P:k * P + P], m.ident[:])
                last.then_inc(v_mm, 1)
                pe.wait_ge(lgT_ok, n + 1)
                if n:
                    pe.wait_ge(lg_ok, TQ * n)
                for k in range(TQ):
                    last = pe.transpose(bank[7][:, k * NLOG:(k + 1) * NLOG], lgT[:, k * P:k * P + P],
                                        m.ident[0:NLOG, 0:NLOG])
                last.then_inc(lg_mm, 1)

            for s in range(6):
                if s < 4:
                    turn_x(s)
                if 1 <= s <= 4:
                    jobs(s - 1)
                if s >= 2:
                    post(s - 2)


def layer0_mix(nc, a, m, bank, bank2):
    with ExitStack() as ctx:
        def sb(name, shape, dt=F32):
            return ctx.enter_context(nc.sbuf_tensor(name, shape, dt))

        def sem(name):
            return ctx.enter_context(nc.semaphore(name))

        UQ = 4
        UNITS = NT // UQ
        PREP = 2 * KV_HEADS
        LOGS_BLOCK = 8
        PARTS = 2
        MIX_SLOTS = NT + 5
        MIX_POOL = 9

        Z, K, T = (sb(n, [P, NT, NS, NS]) for n in ("sk_z", "sk_k", "sk_t"))
        sm, row, col, lrow, lcol, u, v = (sb(n, [P, NT, NS]) for n in ("sk_s", "sk_row", "sk_col", "sk_lr", "sk_lc", "sk_u", "sk_v"))
        rw = sb("rw", [P, NT, 2, NS])
        rws, rwm = sb("rw_s", [P, NT, 2]), sb("rw_m", [P, NT, 2])
        gate = sb("gate", [P, 4])
        y = sb("y", [P, NT, D])
        wbr, wo0 = sb("wbr", [P, D]), sb("wo0", [P, HID])
        probs = sb("probs0", [P, 2, UQ, S])
        PT_SLOTS = 3
        pT = sb("pT0", [P, PT_SLOTS, 512])
        oT = sb("oT0", [P, 512])
        nmax, rsum, rinv = sb("nmax0", [P, NT, 2]), sb("rsum0", [P, NT]), sb("rinv0", [P, NT])
        raw = sb("wraw", [P, 2, REP, HID])
        turned = sb("wturned", [P, 2, REP * HID])
        mixing = sb("mixing", [P, NS, D])
        shares = probs[:].rearrange("p a b c -> p (a b c)").rearrange("p (t n c) -> p t n c", t=NT, n=NS)
        xn, x1 = m.xn0, m.acc

        w_in, gate_ok = sem("b_w_in"), sem("b_gate")
        raw_in = [sem(f"b_raw_in{i}") for i in range(2)]
        prep_mm, prep_copy = sem("b_prepmm"), sem("b_prepcopy")
        stored = [sem(f"b_stored{i}") for i in range(2)]
        chain, chain_act = sem("b_chain"), sem("b_chainact")
        scaled, summed, factor_ok = ([sem(f"b_{n}{i}") for i in range(PARTS)] for n in ("scaled", "summed", "factor"))
        k_ok, factors, logs_ok, z_ok, mix_ok = sem("b_k"), sem("b_factors"), sem("b_logs"), sem("b_z"), sem("b_mix")
        xp_ok, xp_mm, xpT_ok, y_mm, y_ok = (sem("b_" + n) for n in ("xp", "xpmm", "xpT", "ymm", "y"))
        s_mm, smax, p_exp, p_inv = (sem("b_" + n) for n in ("smm", "smax", "pexp", "pinv"))
        t_mm, t_ok, pv_mm = (sem("b_" + n) for n in ("tmm", "t", "pv"))
        o_ok, wo_mm, x1_ok, mixed, pool_mixed = (sem("b_" + n) for n in ("o", "womm", "x1", "mixed", "poolmixed"))

        RW_STEPS, HEAD_STEPS = 5, 11

        TURNS, WEIGHS = ((0, 1, 2), (3, 4), (5, 6), (7,)), ((0,), (1, 2), (3, 4), (5, 6, 7))

        rows = lambda x: x[:]
        cols = lambda x: x[:].rearrange("p t i j -> p t j i")
        over_rows = lambda x: x[:].unsqueeze(3).to_broadcast([P, NT, NS, NS])
        over_cols = lambda x: x[:].unsqueeze(2).to_broadcast([P, NT, NS, NS])

        def part_of(x, k):
            return x[:, k * (NT // PARTS):(k + 1) * (NT // PARTS)]

        def wide_rows(x):
            return x.unsqueeze(3).to_broadcast([P, NT // PARTS, NS, NS])

        def wide_cols(x):
            return x.unsqueeze(2).to_broadcast([P, NT // PARTS, NS, NS])

        def turned_part(x):
            return x.rearrange("p t i j -> p t j i")

        CHUNKS = (SINKHORN_ITERS - 1 - SINKHORN_CHUNK, SINKHORN_CHUNK)

        block = ctx.enter_context(nc.Block())

        @block.sync
        def _(sp):
            sp.dma_start(wbr[:], a["L0_ffn_W_branch"]).then_inc(w_in, 16)
            sp.dma_start(wo0[:], a["L0_attn_Wo"]).then_inc(w_in, 16)
            sp.dma_start(gate[:, 0:1], a["L0_ffn_gate"].partition_broadcast(P)).then_inc(w_in, 16)
            for w in range(PREP + 1):
                if w < PREP:
                    g = w // 2
                    if w >= 2:
                        sp.wait_ge(prep_mm, REP * (w - 1))
                    src = (a["L1_attn_Wq"][g * REP * D:(g + 1) * REP * D, :] if w % 2 == 0
                           else a["L1_attn_Wo"][:, g * REP * D:(g + 1) * REP * D])
                    sp.dma_start(raw[:, w % 2, :, :], src.rearrange("(r p) c -> p r c", p=P)).then_inc(raw_in[w % 2], 16)
                if w >= 1:
                    sp.wait_ge(prep_copy, REP * w)
                    dst = (m.wq_s if (w - 1) % 2 == 0 else m.wo_s)[(w - 1) // 2]
                    sp.dma_start(dst.rearrange("p x y -> p (x y)"), turned[:, (w - 1) % 2, :]).then_inc(stored[(w - 1) % 2], 16)
            for i in range(2):
                sp.wait_ge(stored[i], PREP // 2 * 16)

        @block.gpsimd
        def _(pool):
            pool.wait_ge(chain, RW_STEPS)
            for t in range(NT):
                pool.tensor_tensor(shares[:, t, :, :], xn[:, t, :].rearrange("p (n c) -> p n c", n=NS),
                                   rw[:, t, 0, :].unsqueeze(2).to_broadcast([P, NS, D]), ALU.mult).then_inc(xp_ok, 1)
            for part, count in enumerate(CHUNKS):
                pool.wait_ge(k_ok, part + 1)
                have = 2 * CHUNKS[0] * part + part + 1
                with pool.Fori(0, count) as it:
                    for half in range(2):
                        for k in range(PARTS):
                            factor = wide_rows(part_of(row, k)) if half else wide_cols(part_of(col, k))
                            pool.wait_ge(factor_ok[k], it * 2 + (have + half))
                            pool.tensor_tensor(part_of(T, k), part_of(K, k), factor, ALU.mult).then_inc(scaled[k], 1)
            pool.wait_ge(mix_ok, 1)
            n = 0
            for t in range(NT - MIX_POOL, NT):
                x = x1[:, t, :].rearrange("p (i c) -> p i c", i=NS)
                for j in range(NS):
                    if n:
                        pool.wait_ge(pool_mixed, n)
                    stream = xn[:, t, j * D:(j + 1) * D].unsqueeze(1).to_broadcast([P, NS, D])
                    pool.tensor_tensor(mixing[:], stream, T[:, t, :, j].unsqueeze(2).to_broadcast([P, NS, D]),
                                       ALU.mult).then_inc(pool_mixed, 1)
                    pool.wait_ge(pool_mixed, n + 1)
                    pool.tensor_tensor(x, x, mixing[:], ALU.add).then_inc(pool_mixed, 1)
                    n += 2

        @block.vector
        def _(dve):
            done = [0, 0]

            def after(ins):
                done[0] += 1
                ins.then_inc(chain, 1)
                dve.wait_ge(chain, done[0])

            def after_act():
                done[1] += 1
                dve.wait_ge(chain_act, done[1])

            pq = m.logits[:, :, NZ:NLOG].rearrange("p t (k n) -> p t k n", k=2)
            wide = lambda x: x[:].unsqueeze(3).to_broadcast([P, NT, 2, NS])
            after(dve.tensor_reduce(rwm[:], pq, AX.X, ALU.max))
            after(dve.tensor_tensor(rw[:], pq, wide(rwm), ALU.subtract))
            after_act()
            after(dve.tensor_reduce(rws[:], rw[:], AX.X, ALU.add))
            after(dve.reciprocal(rwm[:], rws[:]))
            after(dve.tensor_tensor(rw[:], rw[:], wide(rwm), ALU.mult))
            dve.wait_ge(gate_ok, 1)
            after(dve.tensor_scalar(gate[:, 1:2], gate[:, 1:2], 1.0, None, ALU.add))
            after(dve.reciprocal(gate[:, 2:3], gate[:, 1:2]))
            after(dve.tensor_scalar(gate[:, 3:4], gate[:, 2:3], -1.0, 1.0, ALU.mult, ALU.add))
            after(dve.tensor_scalar(Z[:], m.logits[:, :, 0:NZ].rearrange("p t (i j) -> p t i j", i=NS), 1.0 / TAU, None, ALU.mult))
            after(dve.tensor_reduce(u[:], rows(Z), AX.X, ALU.max))
            after(dve.tensor_tensor(T[:], Z[:], over_rows(u), ALU.subtract))
            assert done[0] == HEAD_STEPS

            after_act()
            after(dve.tensor_reduce(sm[:], rows(T), AX.X, ALU.add))
            after_act()
            after(dve.tensor_tensor(u[:], u[:], lrow[:], ALU.add))
            after(dve.tensor_tensor(Z[:], Z[:], over_rows(u), ALU.subtract))
            after(dve.tensor_reduce(v[:], cols(Z), AX.X, ALU.max))
            after(dve.tensor_tensor(T[:], Z[:], over_cols(v), ALU.subtract))
            after_act()
            after(dve.tensor_reduce(sm[:], cols(T), AX.X, ALU.add))
            after_act()
            after(dve.tensor_tensor(v[:], v[:], lcol[:], ALU.add))
            after(dve.tensor_tensor(Z[:], Z[:], over_cols(v), ALU.subtract))
            for part, count in enumerate(CHUNKS):
                before = 2 * CHUNKS[0] * part
                if part:
                    dve.wait_ge(logs_ok, 2)
                    after(dve.tensor_tensor(Z[:], Z[:], over_rows(lrow), ALU.add))
                    dve.tensor_tensor(Z[:], Z[:], over_cols(lcol), ALU.add).then_inc(z_ok, 1)
                for k in range(PARTS):
                    dve.memset(part_of(col, k), 1.0).then_inc(factor_ok[k], 1)
                with dve.Fori(0, count) as it:
                    for half in range(2):
                        n = before + half + 1
                        for k in range(PARTS):
                            by = turned_part(part_of(T, k)) if half else part_of(T, k)
                            dve.wait_ge(scaled[k], it * 2 + n)
                            dve.tensor_reduce(part_of(sm, k), by, AX.X, ALU.add).then_inc(summed[k], 1)
                            dve.wait_ge(summed[k], it * 2 + n)
                            dve.reciprocal(part_of(col if half else row, k), part_of(sm, k)).then_inc(factor_ok[k], 1)
                for k in range(PARTS):
                    dve.wait_ge(factor_ok[k], before + part + 1 + 2 * count)
                if part == 0:
                    dve.sem_inc(factors, 1)
            after(dve.tensor_tensor(T[:], K[:], over_rows(row), ALU.mult))
            after(dve.tensor_tensor(T[:], T[:], over_cols(col), ALU.mult))
            mix = T[:].rearrange("p t i j -> p t (i j)")
            after(dve.tensor_scalar(mix, mix, gate[:, 2:3], None, ALU.mult))
            dve.tensor_scalar(mix[:, :, 0:NZ:NS + 1], mix[:, :, 0:NZ:NS + 1], gate[:, 3:4], None, ALU.add).then_inc(mix_ok, 1)
            dve.wait_ge(mix_ok, 1)

            mixes = [0]

            last_op = {t: (mix_ok, 1) for t in range(NT - MIX_POOL)}
            last_op.update({NT - MIX_POOL + k: (pool_mixed, 2 * NS * (k + 1)) for k in range(MIX_POOL)})

            def add_term(t, j):
                if j == NS:
                    dve.wait_ge(y_ok, t // 4 + 1)
                dve.wait_ge(*last_op[t])
                for i in range(NS):
                    cols = slice(i * D, i * D + D)
                    dve.scalar_tensor_tensor(out=x1[:, t, cols], in0=xn[:, t, j * D:(j + 1) * D] if j < NS else y[:, t, :],
                                             scalar=T[:, t, i, j:j + 1] if j < NS else rw[:, t, 1, i:i + 1], in1=x1[:, t, cols],
                                             op0=ALU.mult, op1=ALU.add).then_inc(mixed, 1)
                mixes[0] += NS
                last_op[t] = mixed, mixes[0]

            own = range(NT - MIX_POOL)
            terms = [(t, j) for k in range(0, len(own), 2) for j in range(NS + 1) for t in own[k:k + 2]]
            terms += [(t, NS) for t in range(NT - MIX_POOL, NT)]

            def maximum(t):
                dve.wait_ge(s_mm, t + 1)
                dve.tensor_reduce(nmax[:, t, 0:1], bank2[2 + 2 * (t % 2)], AX.X, ALU.max, negate=True).then_inc(smax, 1)
                dve.wait_ge(smax, 2 * t + 1)
                dve.tensor_scalar(nmax[:, t, 1:2], nmax[:, t, 0:1], SCALE, None, ALU.mult).then_inc(smax, 1)

            def invert(t):
                dve.wait_ge(p_exp, t + 1)
                dve.reciprocal(rinv[:, t:t + 1], rsum[:, t:t + 1]).then_inc(p_inv, 1)

            for unit in range(UNITS + 1):
                if unit < UNITS:
                    for t in range(UQ * unit, UQ * unit + UQ):
                        maximum(t)
                        if t % UQ:
                            invert(t - 1)
                        for term in terms[len(terms) * t // MIX_SLOTS:len(terms) * (t + 1) // MIX_SLOTS]:
                            add_term(*term)
                    invert(UQ * unit + UQ - 1)
                else:
                    for term in terms[len(terms) * NT // MIX_SLOTS:]:
                        add_term(*term)
                if unit:
                    for t in range(UQ * unit - UQ, UQ * unit):
                        dve.wait_ge(wo_mm, t + 1)
                        dve.wait_ge(*last_op[t])
                        dve.wait_ge(p_inv, t + 1)
                        dve.scalar_tensor_tensor(out=x1[:, t, :], in0=bank[7 - t % 2][:], scalar=rinv[:, t:t + 1], in1=x1[:, t, :],
                                                 op0=ALU.mult, op1=ALU.add).then_inc(x1_ok, 1)
                        last_op[t] = x1_ok, t + 1

        @block.scalar
        def _(act):
            def chain_step(at, out, in_, func):
                act.wait_ge(chain, at)
                act.activation(out, in_, func).then_inc(chain_act, 1)

            chain_step(2, rw[:], rw[:], ACT.Exp)
            act.wait_ge(w_in, 48)
            act.activation(gate[:, 1:2], gate[:, 0:1], ACT.Exp, scale=-1.0).then_inc(gate_ok, 1)
            at = HEAD_STEPS
            chain_step(at, T[:], T[:], ACT.Exp)
            at += 1
            chain_step(at, lrow[:], sm[:], ACT.Ln)
            chain_step(at + 4, T[:], T[:], ACT.Exp)
            chain_step(at + 5, lcol[:], sm[:], ACT.Ln)
            act.wait_ge(chain, at + 7)
            act.activation(K[:], Z[:], ACT.Exp).then_inc(k_ok, 1)

            for n in range(4):
                quarter = y[:, 4 * n:4 * n + 4, :].rearrange("p t d -> p (t d)")
                act.wait_ge(xp_mm, n + 1)
                act.activation(quarter, bank[6][:], ACT.Copy).then_inc(xpT_ok, 1)
                act.wait_ge(y_mm, n + 1)
                act.activation(quarter, bank[7][:], ACT.Copy).then_inc(y_ok, 1)

            def prep(blocks):
                for w in blocks:
                    for r in range(REP):
                        n = w * REP + r
                        act.wait_ge(prep_mm, n + 1)
                        if r == 0 and w >= 2:
                            act.wait_ge(stored[w % 2], 16 * (w // 2))
                        src = bank[n % 2]
                        if w % 2 == 0:
                            act.activation(turned[:, w % 2, :].rearrange("p (c o) -> p c o", c=CH)[:, :, r * D:(r + 1) * D],
                                           src.rearrange("p (c o) -> p c o", c=CH), ACT.Copy).then_inc(prep_copy, 1)
                        else:
                            act.activation(turned[:, w % 2, r * HID:(r + 1) * HID], src, ACT.Copy).then_inc(prep_copy, 1)

            prep(range(0, LOGS_BLOCK))
            act.wait_ge(factors, 1)
            act.activation(lrow[:], row[:], ACT.Ln).then_inc(logs_ok, 1)
            act.activation(lcol[:], col[:], ACT.Ln).then_inc(logs_ok, 1)
            act.wait_ge(z_ok, 1)
            act.activation(K[:], Z[:], ACT.Exp).then_inc(k_ok, 1)
            prep(range(LOGS_BLOCK, PREP))
            for unit in range(UNITS + 1):
                for qt in range(UQ):
                    if unit:
                        for j in TURNS[qt]:
                            n = TB * (unit - 1) + j
                            act.wait_ge(t_mm, n + 1)
                            if n >= PT_SLOTS:
                                act.wait_ge(pv_mm, n - PT_SLOTS + 1)
                            act.activation(pT[:, n % PT_SLOTS, :], bank[n % 2][:], ACT.Copy).then_inc(t_ok, 1)
                    if unit < UNITS:
                        t = UQ * unit + qt
                        act.wait_ge(smax, 2 * t + 2)
                        act.activation(probs[:, unit % 2, qt, :], bank2[2 + 2 * (t % 2)], ACT.Exp, bias=nmax[:, t, 1:2],
                                       scale=SCALE, accum_out=rsum[:, t:t + 1]).then_inc(p_exp, 1)
                if unit:
                    act.wait_ge(pv_mm, TB * unit)
                    act.activation(oT[:], bank[6][:], ACT.Copy).then_inc(o_ok, 1)

        @block.tensor
        def _(pe):
            for n in range(4):
                pe.wait_ge(xp_ok, 4 * (n + 1))
                if n == 0:
                    pe.wait_ge(w_in, 48)
                for k in range(4):
                    for j in range(NS):
                        last = pe.matmul(bank[6][:, k * P:(k + 1) * P], shares[:, 4 * n + k, j, :], m.ident[:], start=j == 0, stop=j == NS - 1)
                last.then_inc(xp_mm, 1)
                pe.wait_ge(xpT_ok, n + 1)
                if n:
                    pe.wait_ge(y_ok, n)
                for k in range(4):
                    last = pe.matmul(bank[7][:, k * P:(k + 1) * P], y[:, 4 * n + k, :], wbr[:], start=True, stop=True)
                last.then_inc(y_mm, 1)

            for w in range(PREP):
                pe.wait_ge(raw_in[w % 2], 16 * (w // 2 + 1))
                for r in range(REP):
                    n = w * REP + r
                    if n >= 2:
                        pe.wait_ge(prep_copy, n - 1)
                    for c in range(CH):
                        src = raw[:, w % 2, r, c * P:(c + 1) * P] if w % 2 == 0 else raw[:, w % 2, c, r * D:(r + 1) * D]
                        last = pe.transpose(bank[n % 2][:, c * P:(c + 1) * P], src, m.ident[:])
                    last.then_inc(prep_mm, 1)

            for unit in range(UNITS + 1):
                b, bp = unit * UQ // TB, (unit - 1) * UQ // TB
                for qt in range(UQ):
                    if unit < UNITS:
                        t = UQ * unit + qt
                        if t >= 2:
                            pe.wait_ge(p_exp, t - 1)
                        for half in range(2):
                            ks = slice(b * S + 512 * half, b * S + 512 * half + 512)
                            last = pe.matmul(bank[2 + 2 * (t % 2) + half][:], m.q0[:, t * P:t * P + P], m.k0[:, ks], start=True, stop=True)
                        last.then_inc(s_mm, 1)
                    if unit:
                        def turn(j):
                            n = TB * (unit - 1) + j
                            if n >= 2:
                                pe.wait_ge(t_ok, n - 1)
                            for k in range(UQ):
                                ins = pe.transpose(bank[n % 2][:, k * P:(k + 1) * P], probs[:, (unit - 1) % 2, k, j * P:(j + 1) * P], m.ident[:])
                            ins.then_inc(t_mm, 1)

                        if qt == 0:
                            pe.wait_ge(p_exp, UQ * unit)
                            pe.wait_ge(prep_copy, REP * PREP)
                            turn(0)
                            turn(1)
                        for j in WEIGHS[qt]:
                            n = TB * (unit - 1) + j
                            pe.wait_ge(t_ok, n + 1)
                            if j == 0 and unit > 1:
                                pe.wait_ge(x1_ok, UQ * (unit - 1))
                            pe.matmul(bank[6][:], m.v0[:, bp * TB + j, :], pT[:, n % PT_SLOTS, :], start=j == 0,
                                      stop=j == TB - 1).then_inc(pv_mm, 1)
                            if j + 2 < TB:
                                turn(j + 2)
                if unit:
                    pe.wait_ge(o_ok, unit)
                    for t in range(UQ * unit - UQ, UQ * unit):
                        if t >= 2:
                            pe.wait_ge(x1_ok, t - 1)
                        qs = slice(t % UQ * P, t % UQ * P + P)
                        pe.matmul(bank[7 - t % 2][:], oT[:, qs], wo0[:], start=True, stop=True).then_inc(wo_mm, 1)


def layer1_ffn(nc, a, m, bank):
    with ExitStack() as ctx:
        def sb(name, shape, dt=F32):
            return ctx.enter_context(nc.sbuf_tensor(name, shape, dt))

        def pair(name, shape):
            return sb(name + "_h", shape, F32R), sb(name + "_l", shape, F32R)

        def sem(name):
            return ctx.enter_context(nc.semaphore(name))

        TQ = 4
        xn, x1 = sb("xn1", [P, NT, HID]), m.acc
        wf_raw = sb("wf_raw", [P, CH, HID])
        wf_h, wf_l = pair("wf", [P, CH, HID])
        gw1_raw = sb("gw1_raw", [GH, HID])
        gw1_h, gw1_l = pair("gw1", [P, CH, P])
        la_raw = sb("la_raw", [P, CH, EXP, RANK])
        la_h, la_l = pair("la", [P, CH, P])
        lb_raw = sb("lb_raw", [P, HID])
        lb_h, lb_l = pair("lb", [P, HID])
        gb1 = sb("gb1", [GH, 1])
        gamma, beta = sb("gamma", [P, GH]), sb("beta", [P, GH])
        gw2, gb2 = sb("gw2", [P, EXP, GH]), sb("gb2", [P, EXP])
        st, mv = sb("st1", [P, NT, 6]), sb("mv1", [P, NT, 2])
        veps, rstd, mhalf = sb("veps1", [P, NT]), sb("rstd1", [P, NT]), sb("mhalf1", [P, NT])
        tmpT = sb("tmpT", [P, N])
        hT = sb("hT", [GH, 512])
        h, hs = sb("h", [P, NT, GH]), sb("hs", [P, NT, GH])
        hstat = sb("hstat", [P, 3, NT])
        gates, score, rev = sb("gates", [P, NT, EXP]), sb("score", [P, NT, EXP]), sb("rev", [P, NT, EXP])
        pick = sb("pick", [P, NT, TOPK, EXP])
        top, best = sb("top", [P, TOPK, NT]), sb("best", [P, NT])
        tg = sb("tg", [P, TOPK, NT])
        counts, allowed = sb("counts", [P, TOPK * EXP]), sb("allowed", [P, TOPK, EXP])
        w = sb("w", [P, NT, EXP])
        wexp = sb("wexp", [P, TQ, EXP, RANK])
        tw = sb("tw", [P, 512])
        tw_h, tw_l = pair("twp", [P, 512])

        w_in, const, w_hi, w_lo = sem("c_w_in"), sem("c_const"), sem("c_whi"), sem("c_wlo")
        wt_mm, wt_hi, wt_lo = sem("c_wtmm"), sem("c_wthi"), sem("c_wtlo")
        st_done, mv_done, var_eps, rstd_ok, xn_ok = sem("c_st"), sem("c_mv"), sem("c_var"), sem("c_rstd"), sem("c_xn")
        xT_mm, xT_hi, xT_lo = sem("c_xTmm"), sem("c_xThi"), sem("c_xTlo")
        h_mm, hT_ok, ht_mm, h_ok, lr_mm, lr_ok = (sem("c_" + n) for n in ("hmm", "hT", "htmm", "h", "lrmm", "lr"))
        main_mm, main_ok = sem("c_main"), sem("c_mainok")
        chain, hvar, hrstd, diff, ediff, cnt_mm = (sem("c_" + n) for n in ("chain", "hvar", "hrstd", "diff", "ediff", "cnt"))
        wx_ok, wx_mm, tw_ok, tw_hi, tw_lo, lora_mm, lora_ok = (
            sem("c_" + n) for n in ("wx", "wxmm", "tw", "twhi", "twlo", "lora", "loraok"))
        spilled = sem("c_spilled")
        W_LOADS = 8 + CH

        block = ctx.enter_context(nc.Block())

        @block.sync
        def _(sp):
            loads = [(wf_raw[:], a["L1_ffn_weight"].rearrange("(r p) i -> p r i", p=P)), (gw1_raw[:], a["L1_ffn_gw1"]),
                     (lb_raw[:], a["L1_ffn_lora_B"].rearrange("e r o -> (e r) o")),
                     (gb1[:], a["L1_ffn_gb1"].rearrange("(g o) -> g o", o=1)),
                     (gamma[:], a["L1_ffn_ln_gamma"].partition_broadcast(P)),
                     (beta[:], a["L1_ffn_ln_beta"].partition_broadcast(P)),
                     (gw2[:].rearrange("p e g -> p (e g)"), a["L1_ffn_gw2"].rearrange("e g -> (e g)").partition_broadcast(P)),
                     (gb2[:], a["L1_ffn_gb2"].partition_broadcast(P))]
            loads += [(la_raw[:, c, :, :], a["L1_ffn_lora_A"][:, c * P:(c + 1) * P, :].rearrange("e p r -> p e r"))
                      for c in range(CH)]
            for dst, src in loads:
                sp.dma_start(dst, src).then_inc(w_in, 16)
            sp.wait_ge(xT_lo, NT)
            for k, part in enumerate((m.xT_h, m.xT_l)):
                sp.dma_start(m.xT_s[:, k, :, :], f32(part[:, :, S:N])).then_inc(spilled, 16)
            sp.wait_ge(spilled, 32)

        @block.gpsimd
        def _(pool):
            pool.memset(mhalf[:], -0.5).then_inc(const, 1)
            pool.memset(f32(gw1_h[:]), 0.0).then_inc(const, 1)
            pool.memset(f32(gw1_l[:]), 0.0).then_inc(const, 1)
            for e in range(EXP):
                pool.memset(rev[:, :, e:e + 1], float(EXP - e)).then_inc(const, 1)
            pool.wait_ge(const, 3 + EXP)
            for n in range(4):
                cols = slice(TQ * n, TQ * n + TQ)
                pool.wait_ge(mv_done, TQ * (n + 1))
                pool.tensor_scalar(veps[:, cols], mv[:, cols, 1], 1.0, LN_EPS, ALU.mult, ALU.add).then_inc(var_eps, 1)
                pool.wait_ge(var_eps, n + 1)
                pool.tensor_tensor(rstd[:, cols], veps[:, cols], mhalf[:, cols], ALU.pow).then_inc(rstd_ok, 1)
                if n == 0:
                    pool.wait_ge(w_hi, 2)
                    pool.tensor_tensor(la_l[:], la_raw[:].rearrange("p c e r -> p c (e r)"), f32(la_h[:]), ALU.subtract).then_inc(w_lo, 1)
                    pool.tensor_tensor(lb_l[:], lb_raw[:], f32(lb_h[:]), ALU.subtract).then_inc(w_lo, 1)
            pool.wait_ge(hvar, 1)
            pool.tensor_tensor(hstat[:, 2, :], hstat[:, 1, :], mhalf[:], ALU.pow).then_inc(hrstd, 1)

        @block.vector
        def _(dve):
            steps = [0]

            def after(ins):
                steps[0] += 1
                ins.then_inc(chain, 1)
                dve.wait_ge(chain, steps[0])

            def stats(n):
                for t in range(TQ * n, TQ * n + TQ):
                    dve.bn_stats(st[:, t, :], x1[:, t, :]).then_inc(st_done, 1)
                for t in range(TQ * n, TQ * n + TQ):
                    dve.wait_ge(st_done, t + 1)
                    dve.bn_aggr(mv[:, t, :], st[:, t, :]).then_inc(mv_done, 1)

            def norm(n):
                dve.wait_ge(rstd_ok, n + 1)
                dve.wait_ge(mv_done, TQ * n + TQ)
                for t in range(TQ * n, TQ * n + TQ):
                    dve.tensor_scalar(xn[:, t, :], x1[:, t, :], mv[:, t, 0:1], rstd[:, t:t + 1], ALU.subtract,
                                      ALU.mult).then_inc(xn_ok, 1)

            def low_xT(n):
                for t in range(TQ * n, TQ * n + TQ):
                    dve.wait_ge(xT_hi, t + 1)
                    cols = slice(t * P, t * P + P)
                    dve.tensor_tensor(m.xT_l[:, :, cols], bank[t % 2][:].rearrange("p (c t) -> p c t", c=CH),
                                      f32(m.xT_h[:, :, cols]), ALU.subtract).then_inc(xT_lo, 1)

            def add_main(n):
                for t in range(TQ * n, TQ * n + TQ):
                    dve.wait_ge(main_mm, t + 1)
                    dve.wait_ge(xn_ok, t + 1)
                    dve.tensor_tensor(x1[:, t, :], x1[:, t, :], bank[4 + t % 2][:], ALU.add).then_inc(main_ok, 1)

            def hidden(n):
                dve.wait_ge(ht_mm, n + 1)
                dve.tensor_copy(h[:, TQ * n:TQ * n + TQ, :], bank[7][:, 0:TQ * GH].rearrange("p (t g) -> p t g", t=TQ)).then_inc(h_ok, 1)

            stats(0)
            for n in range(4):
                if n < 3:
                    stats(n + 1)
                norm(n)
                if n == 0:
                    dve.wait_ge(wt_hi, 1)
                    dve.tensor_tensor(gw1_l[:, :, 0:GH], bank[7][:, 0:CH * GH].rearrange("p (c g) -> p c g", c=CH),
                                      f32(gw1_h[:, :, 0:GH]), ALU.subtract).then_inc(wt_lo, 1)
                    for r in range(CH):
                        dve.wait_ge(wt_hi, r + 2)
                        cols = slice(r * P, r * P + P)
                        dve.tensor_tensor(wf_l[:, :, cols], bank[4 + r % 2][:].rearrange("p (c o) -> p c o", c=CH),
                                          f32(wf_h[:, :, cols]), ALU.subtract).then_inc(wt_lo, 1)
                low_xT(n)
                if n:
                    hidden(n - 1)
                    add_main(n - 1)
            hidden(3)
            wide = lambda x: x.unsqueeze(2).to_broadcast([P, NT, GH])
            along = lambda x: x[:].unsqueeze(1).to_broadcast([P, NT, GH])
            dve.wait_ge(h_ok, 4)
            after(dve.tensor_reduce(hstat[:, 0, :], h[:], AX.X, ALU.add))
            after(dve.tensor_scalar(hstat[:, 0, :], hstat[:, 0, :], 1.0 / GH, None, ALU.mult))
            after(dve.tensor_tensor(h[:], h[:], wide(hstat[:, 0, :]), ALU.subtract))
            after(dve.tensor_tensor(hs[:], h[:], h[:], ALU.mult))
            after(dve.tensor_reduce(hstat[:, 1, :], hs[:], AX.X, ALU.add))
            dve.tensor_scalar(hstat[:, 1, :], hstat[:, 1, :], 1.0 / GH, LN_EPS, ALU.mult, ALU.add).then_inc(hvar, 1)
            add_main(3)
            dve.wait_ge(hrstd, 1)
            after(dve.tensor_tensor(h[:], h[:], wide(hstat[:, 2, :]), ALU.mult))
            after(dve.tensor_tensor(h[:], h[:], along(gamma), ALU.mult))
            after(dve.tensor_tensor(h[:], h[:], along(beta), ALU.add))
            after(dve.tensor_scalar(h[:], h[:], 0.0, None, ALU.max))
            for e in range(EXP):
                after(dve.tensor_tensor(hs[:], h[:], gw2[:, e, :].unsqueeze(1).to_broadcast([P, NT, GH]), ALU.mult))
                after(dve.tensor_reduce(gates[:, :, e], hs[:], AX.X, ALU.add))
            after(dve.tensor_tensor(gates[:], gates[:], gb2[:].unsqueeze(1).to_broadcast([P, NT, EXP]), ALU.add))
            bc = lambda x: x.unsqueeze(2).to_broadcast([P, NT, EXP])
            for k in range(TOPK):
                after(dve.tensor_reduce(top[:, k, :], gates[:], AX.X, ALU.max))
                after(dve.tensor_tensor(score[:], gates[:], bc(top[:, k, :]), ALU.is_ge))
                after(dve.tensor_tensor(score[:], score[:], rev[:], ALU.mult))
                after(dve.tensor_reduce(best[:], score[:], AX.X, ALU.max))
                after(dve.tensor_tensor(pick[:, :, k, :], score[:], bc(best[:]), ALU.is_equal))
                if k + 1 < TOPK:
                    after(dve.scalar_tensor_tensor(out=gates[:], in0=pick[:, :, k, :], scalar=-1e38, in1=gates[:],
                                                   op0=ALU.mult, op1=ALU.add))
            dve.tensor_tensor(best[:], top[:, 1, :], top[:, 0, :], ALU.subtract).then_inc(diff, 1)
            dve.tensor_reduce(counts[:], pick[:].rearrange("p t k e -> p (k e) t"), AX.X, ALU.add).then_inc(diff, 1)
            dve.wait_ge(ediff, 1)
            after(dve.tensor_scalar(tg[:, 0, :], tg[:, 1, :], 1.0, None, ALU.add))
            after(dve.reciprocal(tg[:, 0, :], tg[:, 0, :]))
            after(dve.tensor_tensor(tg[:, 1, :], tg[:, 1, :], tg[:, 0, :], ALU.mult))
            dve.wait_ge(cnt_mm, 1)
            after(dve.tensor_scalar(allowed[:].rearrange("p k e -> p (k e)"), bank[6][:, 0:TOPK * EXP], float(CAPACITY), ALPHA,
                                    ALU.is_le, ALU.mult))
            for k in range(TOPK):
                after(dve.tensor_tensor(pick[:, :, k, :], pick[:, :, k, :], bc(tg[:, k, :]), ALU.mult))
                after(dve.tensor_tensor(pick[:, :, k, :], pick[:, :, k, :],
                                        allowed[:, k, :].unsqueeze(1).to_broadcast([P, NT, EXP]), ALU.mult))
            after(dve.tensor_tensor(w[:], pick[:, :, 0, :], pick[:, :, 1, :], ALU.add))
            for n in range(4):
                if n:
                    dve.wait_ge(wx_mm, n)
                dve.tensor_copy(wexp[:], w[:, TQ * n:TQ * n + TQ, :].unsqueeze(3).to_broadcast([P, TQ, EXP, RANK])).then_inc(wx_ok, 1)
                dve.wait_ge(wx_mm, n + 1)
                if n == 0:
                    dve.wait_ge(lr_ok, 4)
                if n:
                    dve.wait_ge(tw_lo, n)
                dve.tensor_tensor(tw[:], tmpT[:, 512 * n:512 * n + 512], bank[0][:], ALU.mult).then_inc(tw_ok, 1)
                dve.wait_ge(tw_hi, n + 1)
                dve.tensor_tensor(tw_l[:], tw[:], f32(tw_h[:]), ALU.subtract).then_inc(tw_lo, 1)
                for t in range(TQ * n, TQ * n + TQ):
                    dve.wait_ge(lora_mm, t + 1)
                    if t == 0:
                        dve.wait_ge(main_ok, NT)
                    dve.tensor_tensor(x1[:, t, :], x1[:, t, :], bank[4 + t % 2][:], ALU.add).then_inc(lora_ok, 1)

        @block.scalar
        def _(act):
            act.wait_ge(const, 3 + EXP)
            act.wait_ge(wt_mm, 1)
            act.activation(gw1_h[:, :, 0:GH], bank[7][:, 0:CH * GH].rearrange("p (c g) -> p c g", c=CH), ACT.Copy).then_inc(wt_hi, 1)
            for r in range(CH):
                act.wait_ge(wt_mm, r + 2)
                act.activation(wf_h[:, :, r * P:(r + 1) * P], bank[4 + r % 2][:].rearrange("p (c o) -> p c o", c=CH),
                               ACT.Copy).then_inc(wt_hi, 1)
            act.wait_ge(w_in, 16 * W_LOADS)
            act.activation(la_h[:], la_raw[:].rearrange("p c e r -> p c (e r)"), ACT.Copy).then_inc(w_hi, 1)
            act.activation(lb_h[:], lb_raw[:], ACT.Copy).then_inc(w_hi, 1)
            for n in range(5):
                if n < 4:
                    for t in range(TQ * n, TQ * n + TQ):
                        act.wait_ge(xT_mm, t + 1)
                        act.activation(m.xT_h[:, :, t * P:t * P + P], bank[t % 2][:].rearrange("p (c t) -> p c t", c=CH),
                                       ACT.Copy).then_inc(xT_hi, 1)
                if n:
                    act.wait_ge(h_mm, n)
                    if n > 1:
                        act.wait_ge(ht_mm, n - 1)
                    act.activation(hT[:], bank[2][0:GH, :], ACT.Identity, bias=gb1[:]).then_inc(hT_ok, 1)
                    act.wait_ge(lr_mm, n)
                    act.activation(tmpT[:, 512 * (n - 1):512 * n], bank[3][:], ACT.Copy).then_inc(lr_ok, 1)
            act.wait_ge(diff, 1)
            act.activation(tg[:, 1, :], best[:], ACT.Exp).then_inc(ediff, 1)
            for n in range(4):
                act.wait_ge(tw_ok, n + 1)
                if n:
                    act.wait_ge(lora_mm, TQ * n)
                act.activation(tw_h[:], tw[:], ACT.Copy).then_inc(tw_hi, 1)

        @block.tensor
        def _(pe):
            pe.wait_ge(w_in, 16 * W_LOADS)
            for c in range(CH):
                last = pe.transpose(bank[7][:, c * GH:(c + 1) * GH], gw1_raw[:, c * P:(c + 1) * P], m.ident[0:GH, 0:GH])
            last.then_inc(wt_mm, 1)
            for r in range(CH):
                if r >= 2:
                    pe.wait_ge(wt_lo, r)
                for c in range(CH):
                    last = pe.transpose(bank[4 + r % 2][:, c * P:(c + 1) * P], wf_raw[:, r, c * P:(c + 1) * P], m.ident[:])
                last.then_inc(wt_mm, 1)

            def turn_x(n):
                for t in range(TQ * n, TQ * n + TQ):
                    pe.wait_ge(xn_ok, t + 1)
                    if t >= 2:
                        pe.wait_ge(xT_lo, t - 1)
                    for c in range(CH):
                        last = pe.transpose(bank[t % 2][:, c * P:(c + 1) * P], xn[:, t, c * P:(c + 1) * P], m.ident[:])
                    last.then_inc(xT_mm, 1)

            def products(n):
                cols = slice(512 * n, 512 * n + 512)
                pe.wait_ge(xT_lo, TQ * (n + 1))
                if n == 0:
                    pe.wait_ge(wt_lo, 1 + CH)
                    pe.wait_ge(w_lo, 2)
                if n:
                    pe.wait_ge(hT_ok, n)
                mm3(pe, bank[2][:], [(gw1_h[:, c, :], gw1_l[:, c, :], m.xT_h[:, c, cols], m.xT_l[:, c, cols])
                                     for c in range(CH)]).then_inc(h_mm, 1)
                if n:
                    pe.wait_ge(lr_ok, n)
                mm3(pe, bank[3][:], [(la_h[:, c, :], la_l[:, c, :], m.xT_h[:, c, cols], m.xT_l[:, c, cols])
                                     for c in range(CH)]).then_inc(lr_mm, 1)
                pe.wait_ge(hT_ok, n + 1)
                if n:
                    pe.wait_ge(h_ok, n)
                for k in range(TQ):
                    last = pe.transpose(bank[7][:, k * GH:(k + 1) * GH], hT[:, k * P:(k + 1) * P], m.ident[0:GH, 0:GH])
                last.then_inc(ht_mm, 1)
                for t in range(TQ * n, TQ * n + TQ):
                    if t >= 2:
                        pe.wait_ge(main_ok, t - 1)
                    ts = slice(t * P, t * P + P)
                    mm3(pe, bank[4 + t % 2][:], [(m.xT_h[:, c, ts], m.xT_l[:, c, ts], wf_h[:, c, :], wf_l[:, c, :])
                                                 for c in range(CH)]).then_inc(main_mm, 1)

            turn_x(0)
            for n in range(4):
                if n < 3:
                    turn_x(n + 1)
                products(n)
            pe.wait_ge(diff, 2)
            pe.matmul(bank[6][:, 0:TOPK * EXP], m.ones[:], counts[:], start=True, stop=True).then_inc(cnt_mm, 1)
            for n in range(4):
                pe.wait_ge(wx_ok, n + 1)
                if n:
                    pe.wait_ge(tw_ok, n)
                for k in range(TQ):
                    last = pe.transpose(bank[0][:, k * P:(k + 1) * P], wexp[:, k, :, :].rearrange("p e r -> p (e r)"), m.ident[:])
                last.then_inc(wx_mm, 1)
                pe.wait_ge(tw_lo, n + 1)
                for t in range(TQ * n, TQ * n + TQ):
                    k = t % TQ
                    pe.wait_ge(main_ok, NT) if t < 2 else pe.wait_ge(lora_ok, t - 1)
                    ts = slice(k * P, k * P + P)
                    mm3(pe, bank[4 + t % 2][:], [(tw_h[:, ts], tw_l[:, ts], lb_h[:], lb_l[:])]).then_inc(lora_mm, 1)


def layer1_keys(nc, a, m, bank):
    with ExitStack() as ctx:
        def sb(name, shape, dt=F32):
            return ctx.enter_context(nc.sbuf_tensor(name, shape, dt))

        def pair(name, shape):
            return sb(name + "_h", shape, F32R), sb(name + "_l", shape, F32R)

        def sem(name):
            return ctx.enter_context(nc.semaphore(name))

        RAWW = 1024
        dn_h, dn_l = pair("dn", [P, CH, KV_HEADS, 2, LAT])
        up_h, up_l = pair("up", [P, 2, LC, KVW])
        cmp_h, cmp_l = pair("cmp", [P, 2 * LC, S])
        raw = sb("kv_raw", [P, 2, RAWW])
        SLOTS = 4
        st_h, st_l = pair("kv_out", [P, SLOTS, 512])
        raw_in = [sem(f"d_raw_in{i}") for i in range(2)]
        first_in = [sem("d_wq_in"), sem("d_wo_in")]
        mm, hi, lo = sem("d_mm"), sem("d_hi"), sem("d_lo")
        stored = [sem(f"d_stored{i}") for i in range(SLOTS)]

        downs = [(pr, n) for pr in range(KV_HEADS // 2) for n in range(2)]
        up_keys = [(n, hk) for n in range(2) for hk in range(KV_HEADS)]
        up_vals = [(j, n) for j in range(TB) for n in range(2)]
        PREP, DOWN, UP = 12, len(downs), len(up_keys) + len(up_vals)
        USES = DOWN + UP
        RAWS = 6
        assert USES % len(bank) == 0

        def per_slot(i):
            return len(range(i, UP, SLOTS))

        block = ctx.enter_context(nc.Block())

        def raw_src(i):
            if i < 2:
                return a[("L1_attn_Wk_down", "L1_attn_Wv_down")[i]].rearrange("(r p) c -> p r c", p=P)
            w = a[("L1_attn_Wk_up", "L1_attn_Wv_up")[i // 2 - 1]]
            return w[(i % 2) * 512:(i % 2) * 512 + 512, :].rearrange("(r p) c -> p r c", p=P)

        @block.sync
        def _(sp):
            for i in range(RAWS):
                if i >= 2:
                    sp.wait_ge(mm, 2 * (i - 1))
                src = raw_src(i)
                sp.dma_start(raw[:, i % 2, :].rearrange("p (r c) -> p r c", r=src.shape[1]), src).then_inc(raw_in[i % 2], 16)
            with sp.Fori(0, B) as b:
                for w in range(UP):
                    sp.wait_ge(lo, b * USES + (PREP + DOWN + w + 1))
                    for k, part in enumerate((st_h, st_l)):
                        src = f32(part[:, w % SLOTS, :])
                        if w < len(up_keys):
                            n, hk = up_keys[w]
                            dst = m.k_s[bass.ds(b * KV_HEADS + hk, 1), :, k, n * 512:n * 512 + 512].rearrange("g p s -> p (g s)")
                        else:
                            j, n = up_vals[w - len(up_keys)]
                            dst = m.v_s[bass.ds(b * KV_HEADS + 4 * n, 4), :, k, j, :].rearrange("g p d -> p g d")
                            src = src.rearrange("p (g d) -> p g d", g=4)
                        sp.dma_start(dst, src).then_inc(stored[w % SLOTS], 16)
            for i in range(SLOTS):
                sp.wait_ge(stored[i], 32 + B * 32 * per_slot(i))

        @block.gpsimd
        def _(pool):
            for i in range(SLOTS):
                pool.memset(f32(st_h[:, i, 0:1]), 0.0).then_inc(stored[i], 32)
            pool.wait_ge(mm, PREP + (B - 1) * USES + DOWN)
            for k, (w, src) in enumerate(((m.wq, m.wq_s), (m.wo, m.wo_s))):
                pool.dma_start(f32(w[:, 1]), src[0]).then_inc(first_in[k], 16)
            for k, loaded in enumerate((m.wq_in, m.wo_in)):
                pool.wait_ge(first_in[k], 16)
                pool.sem_inc(loaded, 16)
            for c in range(CH):
                split_weights(pool, m, m.wq, c, c + 1, m.wq_ok)

        def slices(w):
            return w % SLOTS, w // SLOTS

        def turned_parts(i, bk):
            if i < 4:
                kv, t = i // 2, i % 2
                hs = slice(4 * t, 4 * t + 4)
                return (dn_h[:, :, hs, kv, :], dn_l[:, :, hs, kv, :], bk.rearrange("p (c g e) -> p c g e", c=CH, g=4))
            kv, r, c = (i - 4) // 4, (i - 4) // 2 % 2, i % 2
            cols = slice(r * 512, r * 512 + 512)
            return up_h[:, kv, c, cols], up_l[:, kv, c, cols], bk

        def latent_parts(use, bk):
            pr, n = downs[use]
            for half in range(2):
                for odd in range(2):
                    rows = slice(odd * 64, odd * 64 + 64)
                    cols = slice((2 * pr + half) * P + n * 64, (2 * pr + half) * P + n * 64 + 64)
                    src = bk[half * 64:half * 64 + 64, :].rearrange("p (t r q) -> p r q t", r=4, q=2)[:, :, odd, :]
                    yield cmp_h[rows, :, cols], cmp_l[rows, :, cols], src

        @block.scalar
        def _(act):
            for i in range(PREP):
                act.wait_ge(mm, i + 1)
                high, _, src = turned_parts(i, bank[i % 8])
                act.activation(high, src, ACT.Copy).then_inc(hi, 1)
            with act.Fori(0, B) as b:
                for use in range(USES):
                    bk = bank[(PREP + use) % 8]
                    act.wait_ge(mm, b * USES + (PREP + use + 1))
                    if use < DOWN:
                        for high, _, src in latent_parts(use, bk):
                            last = act.activation(high, src, ACT.Copy)
                        last.then_inc(hi, 1)
                    else:
                        slot, before = slices(use - DOWN)
                        act.wait_ge(stored[slot], b * (32 * per_slot(slot)) + 32 * (before + 1))
                        act.activation(st_h[:, slot, :], bk, ACT.Copy).then_inc(hi, 1)

        @block.vector
        def _(dve):
            for i in range(PREP):
                dve.wait_ge(hi, i + 1)
                high, low, src = turned_parts(i, bank[i % 8])
                dve.tensor_tensor(low, src, f32(high), ALU.subtract).then_inc(lo, 1)
            with dve.Fori(0, B) as b:
                for use in range(USES):
                    bk = bank[(PREP + use) % 8]
                    dve.wait_ge(hi, b * USES + (PREP + use + 1))
                    if use < DOWN:
                        for high, low, src in latent_parts(use, bk):
                            last = dve.tensor_tensor(low, src, f32(high), ALU.subtract)
                        last.then_inc(lo, 1)
                    else:
                        slot, _ = slices(use - DOWN)
                        dve.tensor_tensor(st_l[:, slot, :], bk, f32(st_h[:, slot, :]), ALU.subtract).then_inc(lo, 1)

        @block.tensor
        def _(pe):
            for i in range(PREP):
                if i % 2 == 0:
                    pe.wait_ge(raw_in[i // 2 % 2], 16 * (i // 4 + 1))
                if i >= 8:
                    pe.wait_ge(lo, i - 7)
                block_ = raw[:, i // 2 % 2, :]
                for k in range(4):
                    if i < 4:
                        src = block_[:, (i % 2) * HID + k * P:(i % 2) * HID + k * P + P]
                    else:
                        src = block_[:, k * LATW + (i % 2) * P:k * LATW + (i % 2) * P + P]
                    last = pe.transpose(bank[i % 8][:, k * P:(k + 1) * P], src, m.ident[:])
                last.then_inc(mm, 1)
            with pe.Fori(0, B) as b:
                for use in range(USES):
                    bk = bank[(PREP + use) % 8]
                    pe.wait_ge(lo, b * USES + (PREP + use - 7))
                    if use < DOWN:
                        pr, n = downs[use]
                        if use == 0:
                            pe.wait_ge(lo, PREP)
                        w = lambda x, c: x[:, c, 2 * pr:2 * pr + 2, :, :].rearrange("p g k e -> p (g k e)")
                        x = lambda x, c: x[:, c, bass.ds(b * S + n * 512, 512)]
                        terms = [(w(dn_h, c), w(dn_l, c), x(m.xT_h, c), x(m.xT_l, c)) for c in range(CH)]
                    elif use < DOWN + len(up_keys):
                        n, hk = up_keys[use - DOWN]
                        if hk == 0:
                            pe.wait_ge(lo, b * USES + (PREP + DOWN // 2 * (n + 1)))
                        ks, ts = slice(hk * D, hk * D + D), slice(n * 512, n * 512 + 512)
                        terms = [(up_h[:, 0, c, ks], up_l[:, 0, c, ks], cmp_h[:, c, ts], cmp_l[:, c, ts]) for c in range(LC)]
                    else:
                        j, n = up_vals[use - DOWN - len(up_keys)]
                        ts, vs = slice(j * P, j * P + P), slice(n * 512, n * 512 + 512)
                        terms = [(cmp_h[:, LC + c, ts], cmp_l[:, LC + c, ts], up_h[:, 1, c, vs], up_l[:, 1, c, vs])
                                 for c in range(LC)]
                    mm3(pe, bk, terms).then_inc(mm, 1)


def layer1_attention(nc, a, m, bank, bank2, out):
    with ExitStack() as ctx:
        def sb(name, shape, dt=F32):
            return ctx.enter_context(nc.sbuf_tensor(name, shape, dt))

        def sem(name):
            return ctx.enter_context(nc.semaphore(name))

        HALF = S // 2
        xT = m.xT[:, :, :, 0:S]
        wq, wo, wq_in, wq_ok, wo_in = m.wq, m.wo, m.wq_in, m.wq_ok, m.wo_in
        keys = sb("keys", [P, 2, S], F32R)
        vals = sb("vals", [P, 2, TB, D], F32R)
        q = sb("q", [P, 2, REP, S], F32R)
        probs = sb("probs", [P, 2, REP, S])
        PT_SLOTS = 3
        pT = sb("pT", [P, PT_SLOTS, 2, REP * P], F32R)
        oT = sb("oT", [P, 2, 2, REP * P], F32R)
        free = sb("free", [P, 4])
        nmax, rsum, rinv = (sb(n, [P, TB, REP]) for n in ("nmax", "rsum", "rinv"))

        x_in, k_in, wo_ok = sem("e_x_in"), sem("e_k_in"), sem("e_wo")
        v_in = [sem("e_v_in_low"), sem("e_v_in_high")]
        q_mm, q_hi, q_lo = sem("e_q_mm"), sem("e_q_hi"), sem("e_q_lo")
        s_mm, s_max, p_exp, p_inv, p_ok, p_last = (sem("e_" + n) for n in ("s_mm", "s_max", "p_exp", "p_inv", "p_ok", "p_last"))
        t_mm, t_hi, t_lo, pv_mm = (sem("e_" + n) for n in ("t_mm", "t_hi", "t_lo", "pv_mm"))
        o_hi, o_lo, w_mm, x_add = (sem("e_" + n) for n in ("o_hi", "o_lo", "w_mm", "x_add"))
        stored = sem("e_stored")

        ITERS = B * KV_HEADS
        QS = 2 * REP
        SC = TB * REP
        TILES = TB * (TB + 1) // 2
        T0, PV0, O0, X0 = 2, PT_SLOTS, 1, 1

        def first_tile(u):
            return sum(TB - k for k in range(u))

        T_BANK, O_BANK, W_BANK = 4, 6, 7

        def w_bank(u):
            return bank[W_BANK if u < TB - 2 else T_BANK + u % 2]

        def q_bank(k, first=False):
            if first:
                return bank[k % REP]
            return bank[T_BANK + k if k < REP else W_BANK]

        def q_place(k):
            return k % REP, slice(0, HALF) if k < REP else slice(HALF, S)

        def columns(u):
            n = (TB - u) * P
            off = P if n == 512 + P else 0
            cuts = [0] + ([512 - off] if n + off > 512 else []) + [n]
            return off, n, list(zip(cuts, cuts[1:]))

        LAG = 2

        def steps(last):
            order, due = [], []

            def emit(*step):
                if step[0] == "turn" and step[2] == 0:
                    ours = [d for d in due if d[1][0] in ("probs", "norm") and d[1][1] == step[1]]
                    for d in ours:
                        due.remove(d)
                        order.append(d[1])
                order.append(step)
                for d in due:
                    d[0] -= 1
                while due and due[0][0] <= 0:
                    order.append(due.pop(0)[1])

            def later(n, *step):
                due.append([n, step])
                due.sort(key=lambda d: d[0])

            def flush():
                while due:
                    order.append(due.pop(0)[1])

            def scores(u, h, behind=2, then=2, maximum=0):
                emit("scores", u, h)
                if maximum:
                    later(maximum, "max", u, h)
                else:
                    order.append(("max", u, h))
                later(maximum + behind, "probs", u, h)
                later(maximum + behind + then, "norm", u, h)

            def project(u):
                emit("project", u)
                later(3, "add", u)

            def run(ops):
                for op in ops:
                    emit(*op)

            def query(k, then=1):
                emit("query", k)
                later(then, "qparts", k)

            for h in range(2):
                scores(0, h, 1)
            query(0)
            query(1)
            scores(0, 2, 1)
            scores(0, 3, 1, 1)
            query(2, 2)
            for u in range(1, TB):
                n = TB - u + 1
                turns = [("turn", u - 1, k) for k in range(n)]
                rest = []
                for k in range(n):
                    rest += turns[k + LAG:k + LAG + 1] + [("weigh", u - 1, k)]
                first, second = len(rest) // 3, len(rest) * 2 // 3
                scores(u, 0, 1)
                scores(u, 1)
                if u == 1:
                    order.append(("wo parts", 0))
                if u == 3 and not last:
                    order.append(("wq parts", 0))
                    order.append(("wq parts", 1))
                run(turns[:LAG])
                if u == 1:
                    query(3)
                else:
                    project(u - 2)
                    run(rest[:first] if u < TB - 1 else [])
                if u < TB - 1:
                    scores(u, 2)
                    if u == 1:
                        order.append(("wo parts", 1))
                    if u == 3 and not last:
                        order.append(("wq parts", 2))
                    run(rest[first if u > 1 else 0:second])
                    scores(u, 3)
                    if u == 1:
                        order.append(("wo parts", 2))
                    if u == 3 and not last:
                        order.append(("wq parts", 3))
                    run(rest[second:])
                    if u == 1:
                        order.append(("wo parts", 3))
                else:
                    scores(u, 2)
                    scores(u, 3)
                    run(rest)
                if u == TB - 1:
                    flush()
                emit("heads", u - 1)
                if u >= 4 and not last and u < TB - 1:
                    query(REP + u - 4)
            if not last:
                emit("query", 7)
            emit("turn", u, 0)
            project(u - 1)
            emit("weigh", u, 0)
            emit("heads", u)
            if not last:
                emit("query", 7.5)
                emit("qparts", 7)
            project(u)
            flush()
            return order

        block = ctx.enter_context(nc.Block())

        @block.sync
        def _(sp):
            def load(dst, src):
                return sp.dma_start(f32(dst), src)

            def of_group(t, g):
                return t[bass.ds(g, 1)].rearrange("g p x y -> p (g x) y")

            def of_both(t, bg):
                return t[bass.ds(bg, 1)].rearrange("g p k x y -> p (g k) x y")

            def loads(it, bg, g):
                sp.wait_ge(q_mm, it * QS + QS)
                load(wq[:, 1], of_group(m.wq_s, g)).then_inc(wq_in, 16)
                sp.wait_ge(pv_mm, it * TILES + (PV0 + first_tile(4)))
                load(vals[:, :, 4:8, :], of_both(m.v_s, bg)[:, :, 4:8, :]).then_inc(v_in[1], 16)
                sp.wait_ge(s_mm, it * SC + SC)
                for k in (1, 0):
                    load(keys[:, k, :], m.k_s[bass.ds(bg, 1), :, k, :].rearrange("g p s -> p (g s)")).then_inc(k_in, 16)
                sp.wait_ge(pv_mm, it * TILES + (PV0 + TILES))
                load(vals[:, :, 0:4, :], of_both(m.v_s, bg)[:, :, 0:4, :]).then_inc(v_in[0], 16)
                sp.wait_ge(w_mm, it * TB + TB)
                load(wo[:, 1], of_group(m.wo_s, g)).then_inc(wo_in, 16)

            load(keys[:], m.k_s[0]).then_inc(k_in, 32)
            for half in (1, 0):
                load(vals[:, :, 4 * half:4 * half + 4, :], m.v_s[0, :, :, 4 * half:4 * half + 4, :]).then_inc(v_in[half], 16)
            G = KV_HEADS
            with sp.Fori(0, G - 1) as it:
                loads(it, it + 1, it + 1)
            sp.wait_ge(q_mm, QS * (G - 1) + QS)
            load(xT.rearrange("p k c s -> p (k c) s"), m.xT_s.rearrange("p k c s -> p (k c) s")).then_inc(x_in, 16)
            sp.wait_ge(x_in, 16)
            loads(G - 1, G, 0)
            sp.wait_ge(x_add, X0 + TB * G)
            sp.dma_start(out[0].rearrange("(t p) c -> p t c", p=P), m.acc[:, 0:TB, :]).then_inc(stored, 16)
            with sp.Fori(0, G - 1) as g:
                loads(g + G, g + (G + 1), g + 1)
            for u in range(TB):
                i = TB - 1 - u
                sp.wait_ge(x_add, X0 + TB * (ITERS - 1) + u + 1)
                sp.dma_start(out[1, i * P:i * P + P, :], m.acc[:, TB + i, :]).then_inc(stored, 16)
            sp.wait_ge(stored, 16 * (1 + TB))

        @block.gpsimd
        def _(pool):
            pool.memset(free[:, 0:1], 0.0).then_inc(t_lo, T0)
            pool.memset(free[:, 1:2], 0.0).then_inc(pv_mm, PV0)
            pool.memset(free[:, 2:3], 0.0).then_inc(o_lo, O0)
            pool.memset(free[:, 3:4], 0.0).then_inc(x_add, X0)

            def body(it, last):
                for kind, *arg in steps(last):
                    if kind == "wo parts":
                        pool.wait_ge(wo_in, it * 16 + 16)
                        split_weights(pool, m, wo, arg[0], it * (CH + REP) + (CH + arg[0] + 1), wo_ok)
                    if kind == "wq parts":
                        pool.wait_ge(wq_in, it * 16 + 32)
                        split_weights(pool, m, wq, arg[0], it * (CH + REP) + (CH + REP + arg[0] + 1), wq_ok)
                    if kind == "norm" and arg[1] < REP - 1:
                        u, h = arg
                        p = probs[:, u % 2, h, 0:(TB - u) * P]
                        pool.wait_ge(p_inv, it * SC + (REP * u + h + 1))
                        pool.tensor_tensor(p, p, rinv[:, u, h:h + 1].to_broadcast([P, (TB - u) * P]), ALU.mult).then_inc(p_ok, 1)

            with pool.Fori(0, ITERS - 1) as it:
                body(it, False)
            body(ITERS - 1, True)

        @block.vector
        def _(dve):
            def query_low(k, n, first=False):
                h, cols = q_place(k)
                dve.wait_ge(q_hi, n)
                dve.scalar_tensor_tensor(out=q[:, 1, h, cols], in0=q_bank(k, first), scalar=SCALE, in1=f32(q[:, 0, h, cols]),
                                         op0=ALU.mult, op1=ALU.subtract).then_inc(q_lo, 1)

            def body(it, b, last):
                for kind, *arg in steps(last):
                    u = arg[0]
                    if kind == "max":
                        h = arg[1]
                        off, n, _ = columns(u)
                        dve.wait_ge(s_mm, it * SC + (REP * u + h + 1))
                        dve.tensor_reduce(nmax[:, u, h:h + 1], bank2[2 * (h % 2)][:, off:off + n], AX.X, ALU.max,
                                          negate=True).then_inc(s_max, 1)
                    elif kind == "norm":
                        h = arg[1]
                        dve.wait_ge(p_exp, it * SC + (REP * u + h + 1))
                        dve.reciprocal(rinv[:, u, h:h + 1], rsum[:, u, h:h + 1]).then_inc(p_inv, 1)
                        if h == REP - 1:
                            p = probs[:, u % 2, h, 0:(TB - u) * P]
                            dve.wait_ge(p_inv, it * SC + (REP * u + h + 1))
                            dve.tensor_scalar(p, p, rinv[:, u, h:h + 1], None, ALU.mult).then_inc(p_last, 1)
                    elif kind == "turn":
                        n = first_tile(u) + arg[1]
                        dve.wait_ge(t_hi, it * TILES + (n + 1))
                        dve.tensor_tensor(pT[:, n % PT_SLOTS, 1, :], bank[T_BANK + n % 2], f32(pT[:, n % PT_SLOTS, 0, :]),
                                          ALU.subtract).then_inc(t_lo, 1)
                    elif kind == "heads":
                        dve.wait_ge(o_hi, it * TB + (u + 1))
                        dve.tensor_tensor(oT[:, u % 2, 1, :], bank[O_BANK], f32(oT[:, u % 2, 0, :]), ALU.subtract).then_inc(o_lo, 1)
                    elif kind == "add":
                        x = m.acc[:].rearrange("p (b t) c -> p b t c", b=B)[:, bass.ds(b, 1), TB - 1 - u, :].rearrange("p b c -> p (b c)")
                        dve.wait_ge(w_mm, it * TB + (u + 1))
                        dve.tensor_tensor(x, x, w_bank(u), ALU.add).then_inc(x_add, 1)
                    elif kind == "qparts":
                        query_low(u, it * QS + (REP + u + 1))

            for k in range(REP):
                query_low(REP + k, k + 1, True)
            with dve.Fori(0, ITERS - 1) as it:
                b = nc.s_assert_within(it >> 3, 0, B - 1, skip_runtime_bounds_check_because="it is below 16")
                body(it, b, False)
            body(ITERS - 1, B - 1, True)

        @block.scalar
        def _(act):
            def query_high(k, n, first=False):
                h, cols = q_place(k)
                act.wait_ge(q_mm, n)
                act.activation(q[:, 0, h, cols], q_bank(k, first), ACT.Copy, scale=SCALE).then_inc(q_hi, 1)

            def body(it, last):
                for kind, *arg in steps(last):
                    u = arg[0]
                    if kind == "probs":
                        h = arg[1]
                        off, n, _ = columns(u)
                        act.wait_ge(s_max, it * SC + (REP * u + h + 1))
                        act.activation(probs[:, u % 2, h, 0:n], bank2[2 * (h % 2)][:, off:off + n], ACT.Exp,
                                       bias=nmax[:, u, h:h + 1], accum_out=rsum[:, u, h:h + 1]).then_inc(p_exp, 1)
                    elif kind == "turn":
                        n = first_tile(u) + arg[1]
                        act.wait_ge(pv_mm, it * TILES + (n + 1))
                        act.wait_ge(t_mm, it * TILES + (n + 1))
                        act.activation(pT[:, n % PT_SLOTS, 0, :], bank[T_BANK + n % 2], ACT.Copy).then_inc(t_hi, 1)
                    elif kind == "heads":
                        act.wait_ge(pv_mm, it * TILES + (PV0 + first_tile(u + 1)))
                        act.activation(oT[:, u % 2, 0, :], bank[O_BANK], ACT.Copy).then_inc(o_hi, 1)
                    elif kind == "qparts":
                        query_high(u, it * QS + (REP + u + 1))

            for k in range(REP):
                query_high(REP + k, k + 1, True)
            with act.Fori(0, ITERS - 1) as it:
                body(it, False)
            body(ITERS - 1, True)

        @block.tensor
        def _(pe):
            def queries(k, chunks, first=False):
                h, cols = q_place(k)
                hs = slice(h * D, h * D + D)
                return mm3(pe, q_bank(k, first), [(wq[:, 0, c, hs], wq[:, 1, c, hs], xT[:, 0, c, cols], xT[:, 1, c, cols]) for c in chunks],
                           start=0 in chunks, stop=CH - 1 in chunks)

            def body(it, last):
                for kind, *arg in steps(last):
                    u = arg[0]
                    if kind == "scores":
                        h = arg[1]
                        i = TB - 1 - u
                        e = REP * u + h
                        if e == 0:
                            pe.wait_ge(k_in, it * 32 + 32)
                            pe.wait_ge(q_lo, it * QS + REP)
                        elif e >= 2:
                            pe.wait_ge(p_exp, it * SC + (e - 1))
                        if e == REP * 4:
                            pe.wait_ge(q_lo, it * QS + 2 * REP)
                        off, n, cuts = columns(u)
                        slot = bank2[2 * (h % 2)]
                        qs = slice(i * P, i * P + P)
                        for lo, hi in cuts:
                            mm3(pe, slot[:, off + lo:off + hi], [(q[:, 0, h, qs], q[:, 1, h, qs], keys[:, 0, lo:hi], keys[:, 1, lo:hi])],
                                stop=hi < n)
                        pe.matmul(slot[:, off + n - P:off + n], m.identb[:], m.maskb[:], start=False, stop=True).then_inc(s_mm, 1)
                    elif kind == "turn":
                        k = arg[1]
                        n, j = first_tile(u) + k, TB - 1 - u - k
                        if k == 0:
                            pe.wait_ge(p_ok, it * ((REP - 1) * TB) + (REP - 1) * (u + 1))
                            pe.wait_ge(p_last, it * TB + (u + 1))
                            if u == 0:
                                pe.wait_ge(q_lo, it * QS + (REP + 2))
                        pe.wait_ge(t_lo, it * TILES + (T0 + n - 1))
                        for h in range(REP):
                            ins = pe.transpose(bank[T_BANK + n % 2][:, h * P:(h + 1) * P], probs[:, u % 2, h, j * P:(j + 1) * P], m.ident[:])
                        ins.then_inc(t_mm, 1)
                    elif kind == "weigh":
                        k = arg[1]
                        n, j = first_tile(u) + k, TB - 1 - u - k
                        if k == 0:
                            pe.wait_ge(o_lo, it * TB + (O0 + u))
                            if u == 0:
                                pe.wait_ge(q_lo, it * QS + (REP + 3))
                                for i in range(2):
                                    pe.wait_ge(v_in[i], it * 16 + 16)
                        pe.wait_ge(t_lo, it * TILES + (T0 + n + 1))
                        mm3(pe, bank[O_BANK], [(vals[:, 0, j, :], vals[:, 1, j, :], pT[:, n % PT_SLOTS, 0, :], pT[:, n % PT_SLOTS, 1, :])],
                            start=k == 0, stop=j == 0).then_inc(pv_mm, 1)
                    elif kind == "project":
                        if u == 0:
                            pe.wait_ge(wo_ok, it * REP + REP)
                        pe.wait_ge(o_lo, it * TB + (O0 + u + 1))
                        pe.wait_ge(x_add, it * TB + (X0 + u))
                        if u == 0 or 3 <= u < TB - 2 and not last:
                            pe.wait_ge(q_lo, it * QS + (2 * REP + max(u - 2, 0)))
                        mm3(pe, w_bank(u), [(oT[:, u % 2, 0, h * P:(h + 1) * P], oT[:, u % 2, 1, h * P:(h + 1) * P],
                                             wo[:, 0, h, :], wo[:, 1, h, :]) for h in range(REP)]).then_inc(w_mm, 1)
                    elif kind == "query":
                        if u == 0:
                            pe.wait_ge(x_add, it * TB + X0)
                        elif u == 2:
                            pe.wait_ge(o_lo, it * TB + O0)
                        elif u >= REP:
                            if u == REP:
                                pe.wait_ge(wq_ok, it * CH + 2 * CH)
                            pe.wait_ge(x_add, it * TB + (X0 + int(u) - 1))
                        if u < QS - 1:
                            queries(u, range(CH)).then_inc(q_mm, 1)
                        elif u == QS - 1:
                            queries(u, range(1))
                        else:
                            queries(int(u), range(1, CH)).then_inc(q_mm, 1)

            pe.wait_ge(wq_ok, CH)
            for k in range(REP):
                queries(REP + k, range(CH), True).then_inc(q_mm, 1)
            with pe.Fori(0, ITERS - 1) as it:
                body(it, False)
            body(ITERS - 1, True)
def program(nc, a, out):
    with ExitStack() as ctx:
        def sb(name, shape, dt=F32):
            return ctx.enter_context(nc.sbuf_tensor(name, shape, dt))

        psum = ctx.enter_context(nc.psum_tensor("psum", [P, 8 * 512], F32))
        bank = [psum[:, 512 * i:512 * i + 512] for i in range(8)]
        bank2 = [psum[:, 512 * i:512 * i + 1024] for i in range(7)]
        m = Shared()
        m.acc = sb("acc", [P, NT, HID])
        m.ident = sb("ident", [P, P])
        m.identb = sb("identb", [P, P], BF16)
        m.maskb = sb("maskb", [P, P], BF16)
        m.ones = sb("ones", [P, P])
        m.zero = sb("zero", [P, 1])
        m.wq_s = nc.dram_tensor("wq_parts", (KV_HEADS, P, CH, REP * D), F32, kind="Internal").ap()
        m.wo_s = nc.dram_tensor("wo_parts", (KV_HEADS, P, REP, HID), F32, kind="Internal").ap()
        m.k_s = nc.dram_tensor("k_parts", (B * KV_HEADS, P, 2, S), F32, kind="Internal").ap()
        m.v_s = nc.dram_tensor("v_parts", (B * KV_HEADS, P, 2, TB, D), F32, kind="Internal").ap()
        m.xT_s = nc.dram_tensor("x_parts", (P, 2, CH, S), F32, kind="Internal").ap()
        with ExitStack() as layer0:
            m.xn0 = layer0.enter_context(nc.sbuf_tensor("xn0", [P, NT, HID], F32))
            m.logits = layer0.enter_context(nc.sbuf_tensor("logits", [P, NT, NLOG], F32))
            m.q0 = layer0.enter_context(nc.sbuf_tensor("q0", [P, N], F32))
            m.k0 = layer0.enter_context(nc.sbuf_tensor("k0", [P, N], F32))
            m.v0 = layer0.enter_context(nc.sbuf_tensor("v0", [P, NT, D], F32))
            layer0_project(nc, a, m, bank)
            layer0_mix(nc, a, m, bank, bank2)
        m.xT = sb("xT", [P, 2, CH, N], F32R)
        m.xT_h, m.xT_l = m.xT[:, 0], m.xT[:, 1]
        m.wq = m.xT[:, :, :, S:S + REP * D]
        m.wo = m.xT[:, :, :, S + REP * D:2 * S]
        m.w_hi, m.wq_in, m.wq_ok, m.wo_in = (ctx.enter_context(nc.semaphore(n)) for n in ("w_hi", "wq_in", "wq_ok", "wo_in"))
        layer1_ffn(nc, a, m, bank)
        layer1_keys(nc, a, m, bank)
        layer1_attention(nc, a, m, bank, bank2, out)


_INS = ['L0_attn_x', 'L0_attn_Wqkv', 'L0_attn_bqkv', 'L0_attn_Wo', 'L0_attn_bo', 'L0_ffn_W_res', 'L0_ffn_W_pre',
        'L0_ffn_W_post', 'L0_ffn_H_res_base', 'L0_ffn_H_pre_base', 'L0_ffn_H_post_base', 'L0_ffn_gate',
        'L0_ffn_W_branch', 'L1_attn_Wq', 'L1_attn_Wk_down', 'L1_attn_Wv_down', 'L1_attn_Wk_up', 'L1_attn_Wv_up',
        'L1_attn_Wo', 'L1_ffn_weight', 'L1_ffn_lora_A', 'L1_ffn_lora_B', 'L1_ffn_gw1', 'L1_ffn_gb1',
        'L1_ffn_ln_gamma', 'L1_ffn_ln_beta', 'L1_ffn_gw2', 'L1_ffn_gb2']


def kernel(**inputs):
    import numpy as np
    import concourse.bacc as bacc
    from concourse.bass_utils import run_bass_kernel_spmd

    nc = bacc.Bacc("TRN2", target_bir_lowering=False, num_devices=1)
    arrays, aps = {}, {}
    for name in _INS:
        x = np.ascontiguousarray(inputs[name])
        arrays["in_" + name] = x
        aps[name] = nc.dram_tensor("in_" + name, x.shape, mybir.dt.from_np(x.dtype), kind="ExternalInput").ap()
    out = nc.dram_tensor("out_x", (B, S, HID), F32, kind="ExternalOutput").ap()
    program(nc, aps, out)
    r = run_bass_kernel_spmd(nc, [arrays], core_ids=[0])
    return r.results[0]["out_x"]
```
